# Optimizing a Trainium2 kernel written in Bass

```python
import numpy as np
import jax
import jax.numpy as jnp

def _softmax(x, axis=-1):
    return jax.nn.softmax(x, axis=axis)

def _gelu(x):
    return jax.nn.gelu(x, approximate=True)

def _silu(x):
    return jax.nn.silu(x)

def _sigmoid(x):
    return jax.nn.sigmoid(x)

def _layernorm(x, axis=-1, eps=1e-05):
    m = jnp.mean(x, axis=axis, keepdims=True)
    v = jnp.var(x, axis=axis, keepdims=True)
    return (x - m) / jnp.sqrt(v + eps)

def _scatter_add(tgt, idx, src, axis=0):
    return tgt.at[idx].add(src)

def _segment_sum(src, seg, n):
    return jax.ops.segment_sum(src, seg, n)
kernel_name = 'mk_dlrm_tower_d1_rec_r8_51d1a9'

def setup_inputs(seed: int=0):
    np.random.seed(seed)
    _w = jnp.asarray

    def _rec_inputs():
        import jax
        import jax.numpy as jnp
        _tk = jax.random.key(seed)
        dense_ctx = jax.random.normal(jax.random.fold_in(_tk, 190), (512, 16), jnp.float32)
        ids = jnp.stack([jax.random.randint(jax.random.fold_in(_tk, 200 + f), (512,), 0, v, jnp.int32) for f, v in enumerate([1250, 1250, 1250, 1250, 12500, 1250, 1250, 1250])], axis=1)
        tbl_0 = 0.05 * jax.random.normal(jax.random.fold_in(_tk, 500 + 0), (1250, 1024), jnp.float32)
        tbl_1 = 0.05 * jax.random.normal(jax.random.fold_in(_tk, 500 + 1), (1250, 1024), jnp.float32)
        tbl_2 = 0.05 * jax.random.normal(jax.random.fold_in(_tk, 500 + 2), (1250, 1024), jnp.float32)
        tbl_3 = 0.05 * jax.random.normal(jax.random.fold_in(_tk, 500 + 3), (1250, 1024), jnp.float32)
        tbl_4 = 0.05 * jax.random.normal(jax.random.fold_in(_tk, 500 + 4), (12500, 1024), jnp.float32)
        tbl_5 = 0.05 * jax.random.normal(jax.random.fold_in(_tk, 500 + 5), (1250, 1024), jnp.float32)
        tbl_6 = 0.05 * jax.random.normal(jax.random.fold_in(_tk, 500 + 6), (1250, 1024), jnp.float32)
        tbl_7 = 0.05 * jax.random.normal(jax.random.fold_in(_tk, 500 + 7), (1250, 1024), jnp.float32)
        _rk = jax.random.fold_in(_tk, 7)
        W_top1 = 0.0310087 * jax.random.normal(jax.random.fold_in(_tk, 801), (1040, 512), jnp.float32)
        W_top2 = 0.0441942 * jax.random.normal(jax.random.fold_in(_tk, 802), (512, 256), jnp.float32)
        W_top3 = 0.0625 * jax.random.normal(jax.random.fold_in(_tk, 803), (256, 1), jnp.float32)
        b_top1 = jnp.zeros((512,), jnp.float32)
        b_top2 = jnp.zeros((256,), jnp.float32)
        return (dense_ctx, ids, tbl_0, tbl_1, tbl_2, tbl_3, tbl_4, tbl_5, tbl_6, tbl_7, W_top1, b_top1, W_top2, b_top2, W_top3)
    dense_ctx, ids, tbl_0, tbl_1, tbl_2, tbl_3, tbl_4, tbl_5, tbl_6, tbl_7, W_top1, b_top1, W_top2, b_top2, W_top3 = _rec_inputs()

    def _L0_rec_setup():
        import jax, jax.numpy as jnp
        import numpy as np
        B, F, H = (1024, 8, 1024)

        def _linear_params(key, fan_in, fan_out):
            kw, kb = jax.random.split(key)
            w = jax.random.normal(kw, (fan_in, fan_out), dtype=jnp.float32) * 0.02
            b = jax.random.normal(kb, (fan_out,), dtype=jnp.float32) * 0.02
            return (w, b)
        key = jax.random.key(seed)
        ks = jax.random.split(key, 7)
        field_vectors = jax.random.normal(ks[0], (B, F, H), dtype=jnp.float32)
        Wn1, bn1 = _linear_params(ks[1], H, H)
        Wn2, bn2 = _linear_params(ks[2], H, H)
        Wa1, ba1 = _linear_params(ks[3], 2 * H, H)
        Wa2, ba2 = _linear_params(ks[4], H, H)
        Wo1, bo1 = _linear_params(ks[5], 2 * H, H)
        Wo2, bo2 = _linear_params(ks[6], H, H)
        not_idx = jnp.array([2, 3], dtype=jnp.int64)
        and_pairs = jnp.array([[0, 1], [2, 3]], dtype=jnp.int64)
        or_pairs = jnp.array([[4, 5]], dtype=jnp.int64)
        return {'field_vectors': field_vectors, 'Wn1': Wn1, 'bn1': bn1, 'Wn2': Wn2, 'bn2': bn2, 'Wa1': Wa1, 'ba1': ba1, 'Wa2': Wa2, 'ba2': ba2, 'Wo1': Wo1, 'bo1': bo1, 'Wo2': Wo2, 'bo2': bo2, 'not_idx': not_idx, 'and_pairs': and_pairs, 'or_pairs': or_pairs}
    _L0_rec_all = _L0_rec_setup()
    _L0_rec_in = {k: v for k, v in _L0_rec_all.items() if k in ('Wn1', 'bn1', 'Wn2', 'bn2', 'Wa1', 'ba1', 'Wa2', 'ba2', 'Wo1', 'bo1', 'Wo2', 'bo2', 'not_idx', 'and_pairs', 'or_pairs')}
    del _L0_rec_all
    return {'dense_ctx': dense_ctx, 'ids': ids, 'tbl_0': tbl_0, 'tbl_1': tbl_1, 'tbl_2': tbl_2, 'tbl_3': tbl_3, 'tbl_4': tbl_4, 'tbl_5': tbl_5, 'tbl_6': tbl_6, 'tbl_7': tbl_7, 'W_top1': W_top1, 'b_top1': b_top1, 'W_top2': W_top2, 'b_top2': b_top2, 'W_top3': W_top3, 'L0_rec_Wn1': _L0_rec_in['Wn1'], 'L0_rec_bn1': _L0_rec_in['bn1'], 'L0_rec_Wn2': _L0_rec_in['Wn2'], 'L0_rec_bn2': _L0_rec_in['bn2'], 'L0_rec_Wa1': _L0_rec_in['Wa1'], 'L0_rec_ba1': _L0_rec_in['ba1'], 'L0_rec_Wa2': _L0_rec_in['Wa2'], 'L0_rec_ba2': _L0_rec_in['ba2'], 'L0_rec_Wo1': _L0_rec_in['Wo1'], 'L0_rec_bo1': _L0_rec_in['bo1'], 'L0_rec_Wo2': _L0_rec_in['Wo2'], 'L0_rec_bo2': _L0_rec_in['bo2'], 'L0_rec_not_idx': _L0_rec_in['not_idx'], 'L0_rec_and_pairs': _L0_rec_in['and_pairs'], 'L0_rec_or_pairs': _L0_rec_in['or_pairs']}

def reference(dense_ctx, ids, tbl_0, tbl_1, tbl_2, tbl_3, tbl_4, tbl_5, tbl_6, tbl_7, W_top1, b_top1, W_top2, b_top2, W_top3, L0_rec_Wn1, L0_rec_bn1, L0_rec_Wn2, L0_rec_bn2, L0_rec_Wa1, L0_rec_ba1, L0_rec_Wa2, L0_rec_ba2, L0_rec_Wo1, L0_rec_bo1, L0_rec_Wo2, L0_rec_bo2, L0_rec_not_idx, L0_rec_and_pairs, L0_rec_or_pairs):
    import jax
    import jax.numpy as jnp

    def _L0_rec_ref(field_vectors, Wn1, bn1, Wn2, bn2, Wa1, ba1, Wa2, ba2, Wo1, bo1, Wo2, bo2, not_idx, and_pairs, or_pairs):
        import jax, jax.numpy as jnp
        import numpy as np
        B, F, H = (1024, 8, 1024)

        def _linear_params(key, fan_in, fan_out):
            kw, kb = jax.random.split(key)
            w = jax.random.normal(kw, (fan_in, fan_out), dtype=jnp.float32) * 0.02
            b = jax.random.normal(kb, (fan_out,), dtype=jnp.float32) * 0.02
            return (w, b)
        num_fields = field_vectors.shape[1]
        x_not = jnp.take(field_vectors, not_idx, axis=1)
        t = jnp.tanh(jax.nn.relu(x_not @ Wn1 + bn1) @ Wn2 + bn2)
        iv = field_vectors.at[:, not_idx, :].set(t)

        def pair_fuse(pairs, W1, b1, W2, b2):
            v = jnp.concatenate([jnp.take(iv, pairs[:, 0], axis=1), jnp.take(iv, pairs[:, 1], axis=1)], axis=-1)
            return jax.nn.relu(v @ W1 + b1) @ W2 + b2
        and_out = pair_fuse(and_pairs, Wa1, ba1, Wa2, ba2)
        or_out = pair_fuse(or_pairs, Wo1, bo1, Wo2, bo2)
        processed = jnp.zeros((num_fields,), dtype=field_vectors.dtype).at[and_pairs.reshape(-1)].set(1.0).at[or_pairs.reshape(-1)].set(1.0)
        remaining = 1.0 - processed
        sum_res = and_out.sum(axis=1) + or_out.sum(axis=1) + jnp.einsum('bfh,f->bh', iv, remaining)
        count = and_pairs.shape[0] + or_pairs.shape[0] + remaining.sum()
        return sum_res / count
    e = jnp.stack([tbl_0[ids[:, 0]], tbl_1[ids[:, 1]], tbl_2[ids[:, 2]], tbl_3[ids[:, 3]], tbl_4[ids[:, 4]], tbl_5[ids[:, 5]], tbl_6[ids[:, 6]], tbl_7[ids[:, 7]]], axis=1)
    z = _L0_rec_ref(e, L0_rec_Wn1, L0_rec_bn1, L0_rec_Wn2, L0_rec_bn2, L0_rec_Wa1, L0_rec_ba1, L0_rec_Wa2, L0_rec_ba2, L0_rec_Wo1, L0_rec_bo1, L0_rec_Wo2, L0_rec_bo2, L0_rec_not_idx, L0_rec_and_pairs, L0_rec_or_pairs)
    z = z.reshape(z.shape[0], -1)
    h = jnp.concatenate([z, dense_ctx], axis=1)
    h = jnp.maximum(h @ W_top1 + b_top1, 0.0)
    h = jnp.maximum(h @ W_top2 + b_top2, 0.0)
    y = h @ W_top3
    return y

_drawn_inputs = setup_inputs


def setup_inputs(seed=0):
    import zlib

    import numpy as np

    out = dict(_drawn_inputs(seed))
    spreads = {'b_top1': (0.0, 0.1), 'b_top2': (0.0, 0.1)}
    factors = {'tbl_0': 4.417,
     'tbl_1': 4.463,
     'tbl_2': 8.0,
     'tbl_3': 8.0,
     'tbl_4': 4.546,
     'tbl_5': 4.671,
     'L0_rec_Wn1': 8.0,
     'L0_rec_bn1': 8.0,
     'L0_rec_Wn2': 8.0,
     'L0_rec_bn2': 8.0,
     'L0_rec_Wa1': 2.948,
     'L0_rec_ba1': 3.85,
     'L0_rec_Wo1': 3.478,
     'L0_rec_bo1': 8.0,
     'L0_rec_Wo2': 2.725}
    for name, (base, spread) in spreads.items():
        noise = np.random.default_rng([zlib.crc32(name.encode()), seed]).standard_normal(out[name].shape)
        drawn = base * np.exp(spread * noise) if base else spread * noise
        out[name] = jnp.asarray(drawn.astype(out[name].dtype))
    for name, factor in factors.items():
        out[name] = (out[name] * factor).astype(out[name].dtype)
    return out
```

```python
from contextlib import ExitStack

import concourse.bass as bass
from concourse import mybir

ALU = mybir.AluOpType
ACT = mybir.ActivationFunctionType
AX = mybir.AxisListType
F32 = mybir.dt.float32
F32R = mybir.dt.float32r
I32 = mybir.dt.int32

P = 128
B = 512
H = 1024
KT = H // P
BT = B // P
NF = 8
NSLOT = 8
NPAIR = 3
HALF = H // 2
MB, TB = 4, 4
WR = 4
RR = 2
D1, D2 = 512, 256
KD = 16

S_N1, S_N2, S_PAIR, S_L2, S_T1, S_T2, S_T3 = 0, 16, 32, 80, 88, 92, 94
C_PAIR, C_L2, C_T1, C_T2 = 16, 64, 80, 84
N_CHUNK = 85
U_N1, U_REST, U_SLOT = 8, 16, 24
V_N1, V_N2, V_A1, V_A2, V_O1, V_O2, V_T1, V_T2, V_W3 = 0, 8, 16, 24, 32, 40, 48, 52, 54
NV = 56
SPLIT_AT = {0: 3, 3: 4, 4: 5, 7: 6}
A0_AT = (2, 3, 6, 7)
REST_AT = (3, 3, 2, 3, 3, 2, 0, 0)


def steps_of_not_chunk(c):
    layer, j = divmod(c, KT)
    return 16 * layer + j // 2 * 4 + j % 2 + 3


def program(nc, table, ids, fields, chunks, vectors, dense, w_dense, out, offsets):
    V = table.shape[0]
    chunk_rows = chunks.rearrange("c p n -> (c p) n")
    half_rows = table.rearrange("v (g c) -> (v g) c", g=2)

    with ExitStack() as ctx:
        base = (nc.sbuf_base + 63) // 64 * 64
        used = [base]

        def place(name, shape, dt, at=None):
            size = 4
            for n in shape[1:]:
                size *= n
            if at is None:
                at = used[0]
                used[0] += (size + 31) // 32 * 32
            return nc.alloc_sbuf_tensor_at(name, shape, dt, offset=at)

        SPLIT = 2 * KT * B * 4
        area = [used[0] + i * SPLIT for i in range(4)]
        used[0] += 4 * SPLIT
        at_a, at_b, at_c, at_d = area
        xs = [place("x0_split", [P, 2, KT, B], F32R, at_a), place("x1_split", [P, 2, KT, B], F32R, at_b)]
        us = [place("u0_split", [P, 2, KT, B], F32R, at_c), place("u1_split", [P, 2, KT, B], F32R, at_d)]
        not_out = place("not_out", [P, 2, KT, B], F32, at_a)
        slot_split = [place("slot_even", [P, 2, KT, B], F32R, at_b), place("slot_odd", [P, 2, KT, B], F32R, at_c)]
        or_split = place("or_split", [P, 2, KT, B], F32R, at_a)
        and_split = place("and_split", [P, 2, KT, B], F32R, at_b)
        z_split = place("z_split", [P, 2, KT, B], F32R, at_c)
        rows1 = place("rows_input1", [P, 2, BT, HALF], F32, at_d)
        partial = place("partial", [P, KT, B], F32, at_d)
        and_sum = place("and_sum", [P, KT, B], F32, at_d + SPLIT // 2)
        h1_split = place("h1_split", [P, 2, D1 // P, B], F32R, at_d)
        h2 = place("h2", [P, D2 // P, B], F32, at_d + SPLIT // 2)
        y = place("y", [1, B], F32, at_d + SPLIT // 2 + D2 // P * B * 4)
        at_rows = used[0]
        rows = place("rows", [P, 2, BT, HALF], F32)
        rest_ring = place("rest_ring", [P, 2, H], F32, at_rows)
        rest_acc = place("rest_acc", [P, 2, H], F32, at_rows + 2 * H * 4)
        dense_raw = place("dense_raw", [KD, B + D1], F32, at_rows)
        dense_split = place("dense_split", [KD, 2, B + D1], F32R, at_rows + (B + D1) * 4)
        z_add = place("z_add", [P, KT, B], F32)
        w_raw = place("w_raw", [P, RR, KT * P], F32)
        w_split = place("w_split", [P, WR, 2, KT * P], F32R)
        ident = place("ident", [P, P], F32)
        vec = place("vec", [P, NV], F32)
        z_bias = place("z_bias", [P, KT], F32)
        ids_sb = place("ids_sb", [P, BT, NF], I32)
        fields_i = place("fields_i", [P, NSLOT], I32)
        fields_f = place("fields_f", [P, NSLOT], F32)
        field_no = place("field_no", [P, NF], F32)
        offs = place("offs", [P, NF], F32)
        row_no = place("row_no", [P, BT, NF], F32)
        onehot = place("onehot", [P, NSLOT, NF], F32)
        picked = place("picked", [P, NSLOT, BT, NF], F32)
        slot_row = place("slot_row", [P, NSLOT, BT], F32)
        slot_idx = place("slot_idx", [P, NSLOT, 2, BT], I32)
        is_t0 = place("is_t0", [P, NSLOT], F32)
        is_t1 = place("is_t1", [P, NSLOT], F32)
        skip = place("skip", [P, NSLOT], F32)
        masks = place("masks", [P, NSLOT * 2], I32)
        mask_now = place("mask_now", [P, 2], I32)
        paired = place("paired", [P, NF], F32)
        notted = place("notted", [P, NF], F32)
        remain = place("remain", [P, NF], F32)
        w_row = place("w_row", [P, NF], F32)
        rest_row = place("rest_row", [P, BT, NF], F32)
        rest_idx = place("rest_idx", [P, BT, NF], I32)
        w_not = place("w_not", [P, 2, NF], F32)
        w_t = place("w_t", [P, 2], F32)
        not_same = place("not_same", [P, 1], F32)
        n_rest = place("n_rest", [P, 1], F32)
        inv_count = place("inv_count", [P, 1], F32)
        nc.sbuf_tensor("fence", [P, used[0] - nc.sbuf_base], mybir.dt.uint8).__enter__()

        acc = [ctx.enter_context(nc.psum_tensor(f"acc{i}", [P, B], F32)) for i in range(MB)]
        tps = [ctx.enter_context(nc.psum_tensor(f"tps{i}", [P, BT, P], F32)) for i in range(TB)]

        def sem(name):
            return ctx.enter_context(nc.semaphore(name))

        ids_in = sem("ids_in")
        vec_in = sem("vec_in")
        dense_in = sem("dense_in")
        raw_in = [sem(f"raw_in{i}") for i in range(RR)]
        w_hi = sem("w_hi")
        w_lo = sem("w_lo")
        consts_set = sem("consts_set")
        prep = sem("prep")
        idx_set = sem("idx_set")
        rows_in = [sem(f"rows_in{g}") for g in range(2)]
        rows1_in = [sem(f"rows1_in{g}") for g in range(2)]
        rest_in = [sem(f"rest_in{r}") for r in range(2)]
        rest_summed = sem("rest_summed")
        tr_done = sem("tr_done")
        tr_free = [sem(f"tr_free{i}") for i in range(TB)]
        picked0 = sem("picked0")
        picked1 = sem("picked1")
        op_hi = sem("op_hi")
        mm_done = sem("mm_done")
        acc_free = [sem(f"acc_free{i}") for i in range(MB)]
        hid_hi = sem("hid_hi")
        t_added = sem("t_added")
        mask_set = sem("mask_set")
        sum_zeroed = sem("sum_zeroed")
        pair_in = sem("pair_in")
        and_hi = sem("and_hi")
        and_lo = sem("and_lo")
        or_hi = sem("or_hi")
        z_fin = sem("z_fin")
        z_in = sem("z_in")
        z_hi = sem("z_hi")
        dense_hi = sem("dense_hi")
        dense_lo = sem("dense_lo")
        h1_hi = sem("h1_hi")
        y_set = sem("y_set")
        stored = sem("stored")

        block = ctx.enter_context(nc.Block())

        @block.sync
        def _(sp):
            sp.dma_start(ids_sb[:], ids.rearrange("(t p) f -> p t f", p=P)).then_inc(ids_in, 16)
            sp.dma_start(fields_i[:], fields.partition_broadcast(P)).then_inc(ids_in, 16)

            def load(chunk, c, r, first=False):
                if not first:
                    sp.wait_ge(w_lo, c - 1)
                sp.dma_start(w_raw[:, r, :], chunk_rows[bass.ds(chunk * P, P), :]).then_inc(raw_in[r], 16)

            load(0, 0, 0, first=True)
            load(1, 1, 1, first=True)
            sp.dma_start(vec[:], vectors).then_inc(vec_in, 16)
            with sp.Fori(1, 16) as i:
                for r in range(RR):
                    load(i * 2 + r, i * 2 + r, r)
            with sp.Fori(16, 40) as i:
                for r in range(RR):
                    load(i * 2 + (r - 16), i * 2 + r, r)
            for c in range(80, N_CHUNK):
                load(c - 16, c, c % RR)
            sp.wait_ge(y_set, 1)
            sp.dma_start(out.rearrange("b o -> o b"), y[:]).then_inc(stored, 16)
            sp.wait_ge(stored, 16)

        @block.gpsimd
        def _(pool):
            for f in range(NF):
                pool.memset(offs[:, f:f + 1], float(offsets[f]))
                pool.memset(field_no[:, f:f + 1], float(f))
            pool.memset(ident[:], 0.0).then_inc(consts_set, 1)
            pool.wait_ge(consts_set, 1)
            pool.affine_select(out=ident[:], in_=ident[:], compare_op=ALU.not_equal, fill=1.0, base=0,
                               pattern=[[-1, P]], channel_multiplier=1).then_inc(consts_set, 1)

            def gather(dst, src, idx, landed):
                pool.indirect_dma_start(dst, None, src, bass.IndirectOffsetOnAxis(ap=idx, axis=0),
                                        bounds_check=src.shape[0] - 1, oob_is_err=False).then_inc(landed, 16)

            pool.wait_ge(idx_set, 1)
            for g in range(2):
                for t in range(BT):
                    gather(rows[:, g, t, :], half_rows, slot_idx[:, 0, g, t:t + 1], rows_in[g])
            for g in range(2):
                for t in range(BT):
                    gather(rows1[:, g, t, :], half_rows, slot_idx[:, 1, g, t:t + 1], rows1_in[g])
            pool.wait_ge(idx_set, 2)
            pool.wait_ge(tr_done, KT)
            for n in range(BT * NF):
                if n >= 2:
                    pool.wait_ge(rest_summed, n - 1)
                gather(rest_ring[:, n % 2, :], table, rest_idx[:, n // NF, n % NF:n % NF + 1], rest_in[n % 2])
            pool.wait_ge(tr_done, U_SLOT)

            for s in range(2 * NPAIR):
                for g in range(2):
                    if s >= 1:
                        pool.wait_ge(tr_done, U_SLOT + (s - 1) * KT + 4 * (g + 1))
                    for t in range(BT):
                        gather(rows[:, g, t, :], half_rows, slot_idx[:, 2 + s, g, t:t + 1], rows_in[g])
                if s == 0:
                    pool.wait_ge(mm_done, S_PAIR)
                    pool.memset(and_sum[:], 0.0).then_inc(sum_zeroed, 1)

            pool.wait_ge(tr_done, U_SLOT + 6 * KT)
            pool.dma_start(dense_raw[:, 0:B], dense).then_inc(dense_in, 16)
            pool.dma_start(dense_raw[:, B:B + D1], w_dense).then_inc(dense_in, 16)

        @block.tensor
        def _(pe):
            def unit(src, bank, h):
                for t in range(BT):
                    c = h % 4 * P
                    ins = pe.transpose(tps[bank][:, t, :], src[:, h // 4, t, c:c + P], ident[:])
                ins.then_inc(tr_done, 1)

            def slot_unit(s, h, bank):
                if bank == 0:
                    pe.wait_ge(rows_in[h // 4], s * 64 + 128)
                pe.wait_ge(tr_free[bank], s * 2 + (U_SLOT + h) // 4)
                unit(rows, bank, h)

            def product(bank, w, x, k, wk, start, stop):
                lhs = [w_split[:, w, p, wk * P:(wk + 1) * P] for p in range(2)]
                for n, (a, b) in enumerate(((0, 0), (1, 0), (0, 1))):
                    ins = pe.matmul(acc[bank][:], lhs[a], x[:, b, k, :], start=start and n == 0, stop=stop and n == 2)
                return ins

            pe.wait_ge(consts_set, 2)
            for n in range(U_REST):
                if n % 4 == 0:
                    pe.wait_ge((rows_in if n < KT else rows1_in)[n // 4 % 2], 64)
                if n >= 4:
                    pe.wait_ge(tr_free[n % 4], n // 4)
                unit(rows if n < KT else rows1, n % 4, n % KT)

            for g in range(16):
                u, f, c = g % 8, g % 4 // 2, g % 8 // 4 * 2 + g % 2
                if u in (4, 7):
                    t = g // 8 * 2 + u // 6
                    pe.wait_ge(rest_summed, NF * (t + 1))
                    for q in range(2):
                        n = U_REST + 2 * t + q
                        pe.wait_ge(tr_free[n % TB], n // TB)
                        for h in range(4):
                            ins = pe.transpose(tps[n % TB][:, h, :], rest_acc[:, t % 2, (4 * q + h) * P:(4 * q + h + 1) * P], ident[:])
                        ins.then_inc(tr_done, 1)
                pe.wait_ge(tr_free[TB - 1], 2 * (f + 1))
                pe.wait_ge(w_lo, g // 8 * 4 + c + 1)
                if g >= MB:
                    pe.wait_ge(acc_free[g % MB], g // MB)
                for k in range(KT):
                    ins = product(g % MB, c, xs[f], k, k, k == 0, k == KT - 1)
                ins.then_inc(mm_done, 1)

            for g in range(16):
                u, f, c = g % 8, g % 4 // 2, g % 8 // 4 * 2 + g % 2
                if u in A0_AT:
                    slot_unit(0, g // 8 * 4 + A0_AT.index(u), A0_AT.index(u))
                pe.wait_ge(acc_free[1 + 2 * f], 4)
                pe.wait_ge(w_lo, KT + g // 8 * 4 + c + 1)
                pe.wait_ge(acc_free[u % MB], (S_N2 + g) // MB)
                for k in range(KT):
                    ins = product(u % MB, c, us[f], k, k, k == 0, k == KT - 1)
                ins.then_inc(mm_done, 1)

            def slot_steps(s, par, build):
                for h in range(KT):
                    if build:
                        slot_unit(s + 1, h, h % 4)
                    pe.wait_ge(w_lo, s * KT + (C_PAIR + h + 1))
                    pe.wait_ge(acc_free[h % 4], s * 2 + (S_PAIR + h) // 4)
                    for k in range(KT):
                        if h == 0 and k in (0, 6, 7):
                            n = U_SLOT + max(k, 5)
                            pe.wait_ge(tr_free[n % TB], s * 2 + (n // TB + 1))
                        ins = product(h % 4, h % 4, slot_split[par], k, k, k == 0, k == KT - 1)
                    ins.then_inc(mm_done, 1)

            with pe.Fori(0, 2) as i:
                slot_steps(i * 2, 0, True)
                slot_steps(i * 2 + 1, 1, True)
            slot_steps(4, 0, True)
            slot_steps(5, 1, False)

            with pe.Fori(0, 2) as hh:
                for u in range(4):
                    pe.wait_ge(acc_free[u], hh + S_L2 // 4)
                    for part, x in enumerate((and_split, or_split)):
                        w = 2 * u + part
                        pe.wait_ge(w_lo, hh * 8 + (C_L2 + w + 1))
                        for k in range(KT):
                            if part == 0 and k == 0:
                                pe.wait_ge(and_lo, KT)
                            if part == 1 and k in (0, KT - 1):
                                pe.wait_ge(acc_free[2 + k // (KT - 1)], S_L2 // MB)
                            ins = product(u, w % 4, x, k, k, part + k == 0, part == 1 and k == KT - 1)
                    ins.then_inc(mm_done, 1)

            for j in range(D1 // P):
                pe.wait_ge(w_lo, C_T1 + j + 1)
                pe.wait_ge(acc_free[j], (S_T1 + j) // 4)
                pe.wait_ge(acc_free[2], S_T1 // MB)
                for k in range(KT - 1):
                    product(j, j, z_split, k, k, k == 0, False)
            pe.wait_ge(dense_lo, 1)
            pe.wait_ge(acc_free[3], S_T1 // MB)
            for j in range(D1 // P):
                product(j, j, z_split, KT - 1, KT - 1, False, False)
                for n, (a, b) in enumerate(((0, 0), (1, 0), (0, 1))):
                    ins = pe.matmul(acc[j][:], dense_split[:, a, B + j * P:B + (j + 1) * P], dense_split[:, b, 0:B],
                                    start=False, stop=n == 2)
                ins.then_inc(mm_done, 1)

            K2 = D1 // P
            pe.wait_ge(w_lo, C_T2 + 1)
            for j in range(D2 // P):
                pe.wait_ge(acc_free[j], (S_T2 + j) // 4)
                pe.wait_ge(acc_free[2], S_T2 // MB)
                for k in range(K2 - 1):
                    product(j, C_T2 % WR, h1_split, k, j * K2 + k, k == 0, False)
            pe.wait_ge(acc_free[3], S_T2 // MB)
            for j in range(D2 // P):
                product(j, C_T2 % WR, h1_split, K2 - 1, j * K2 + K2 - 1, False, True).then_inc(mm_done, 1)

            pe.wait_ge(vec_in, 16)
            pe.wait_ge(acc_free[2], (S_T3) // 4)
            for k in range(D2 // P):
                pe.wait_ge(acc_free[k], S_T2 // MB + 1)
                ins = pe.matmul(acc[2][0:1, :], vec[:, V_W3 + k:V_W3 + k + 1], h2[:, k, :], start=k == 0, stop=k == D2 // P - 1)
            ins.then_inc(mm_done, 1)

        @block.scalar
        def _(act):
            def weights_hi(r, rw, landed, steps=None):
                act.wait_ge(raw_in[rw], landed)
                if steps is not None:
                    act.wait_ge(mm_done, steps)
                act.copy(w_split[:, r, 0, :], w_raw[:, rw, :]).then_inc(w_hi, 1)

            def chunk_hi(c, steps=None):
                weights_hi(c % WR, c % RR, 16 * (c // RR + 1), steps)

            def slot_chunk_hi(s, h):
                weights_hi((h + 3) % WR, (h + 3) % RR, s * 64 + 16 * ((C_PAIR + h + 3) // RR + 1),
                           s * KT + (S_PAIR + h))

            def operand_hi(dst, h):
                act.copy(dst[:, 0, h, :], tps[h % TB][:].rearrange("p t b -> p (t b)")).then_inc(op_hi, 1)

            for c in range(3):
                chunk_hi(c)
            for n in range(2 * KT):
                act.wait_ge(tr_done, n + 1)
                operand_hi(xs[n // KT], n % KT)
            act.wait_ge(vec_in, 16)

            for g in range(16):
                u, f, j = g % 8, g % 4 // 2, g // 4 * 2 + g % 2
                if u in SPLIT_AT:
                    c = g // 8 * 4 + SPLIT_AT[u]
                    chunk_hi(c, steps_of_not_chunk(c - WR) if c >= WR else None)
                if u in (4, 7):
                    t = g // 8 * 2 + u // 6
                    for q in range(2):
                        n = U_REST + 2 * t + q
                        act.wait_ge(tr_done, n + 1)
                        act.copy(z_add[:, 4 * q:4 * q + 4, t * P:(t + 1) * P], tps[n % TB][:]).then_inc(tr_free[n % TB], 1)
                act.wait_ge(mm_done, g + 1)
                bias = vec[:, V_N1 + j:V_N1 + j + 1]
                act.activation(us[f][:, 0, j, :], acc[g % MB][:], ACT.Relu, bias=bias)
                act.activation(acc[g % MB][:], acc[g % MB][:], ACT.Relu, bias=bias).then_inc(hid_hi, 1)

            for g in range(16):
                u, f, j = g % 8, g % 4 // 2, g // 4 * 2 + g % 2
                if u in SPLIT_AT:
                    c = KT + g // 8 * 4 + SPLIT_AT[u]
                    chunk_hi(c, steps_of_not_chunk(c - WR))
                act.wait_ge(mm_done, S_N2 + g + 1)
                act.activation(not_out[:, f, j, :], acc[g % MB][:], ACT.Tanh,
                               bias=vec[:, V_N2 + j:V_N2 + j + 1]).then_inc(acc_free[g % MB], 1)
                if u in A0_AT:
                    h = g // 8 * 4 + A0_AT.index(u)
                    act.wait_ge(picked1, h + 1)
                    operand_hi(slot_split[0], h)

            def first_operand(s, bias_at):
                for h in range(KT):
                    slot_chunk_hi(s, h)
                    act.wait_ge(picked1, s * KT + (KT + h + 1))
                    operand_hi(slot_split[1], h)
                    act.wait_ge(mm_done, s * KT + (S_PAIR + h + 1))
                    act.activation(partial[:, h, :], acc[h % MB][:], ACT.Identity,
                                   bias=vec[:, bias_at + h:bias_at + h + 1]).then_inc(acc_free[h % MB], 1)

            with act.Fori(0, 2) as i:
                first_operand(i * 2, V_A1)
                for h in range(KT):
                    slot_chunk_hi(i * 2 + 1, h)
                    act.wait_ge(picked1, i * (2 * KT) + (2 * KT + h + 1))
                    operand_hi(slot_split[0], h)
            first_operand(4, V_O1)
            act.wait_ge(mm_done, S_PAIR + 5 * KT)
            act.wait_ge(acc_free[MB - 1], (S_PAIR + 4 * KT) // MB)
            for h in range(KT):
                if h < KT - 1:
                    slot_chunk_hi(5, h)
                act.copy(and_split[:, 0, h, :], and_sum[:, h, :]).then_inc(and_hi, 1)
                act.wait_ge(pair_in, 2 * KT + h + 1)
                act.activation(or_split[:, 0, h, :], acc[h % MB][:], ACT.Relu).then_inc(or_hi, 1)

            for j in range(KT):
                for c in (C_L2 + 2 + 2 * j, C_L2 + 3 + 2 * j):
                    chunk_hi(c, S_L2 + j)
                if j == 4:
                    act.wait_ge(dense_in, 32)
                    act.copy(dense_split[:, 0, :], dense_raw[:]).then_inc(dense_hi, 1)
                act.wait_ge(z_in, j + 1)
                act.copy(z_split[:, 0, j, :], acc[j % MB][:]).then_inc(z_hi, 1)
            for c in (C_T1 + 2, C_T1 + 3):
                chunk_hi(c, S_T1)
            chunk_hi(C_T2, S_T1 + 1)
            for j in range(D1 // P):
                act.wait_ge(mm_done, S_T1 + j + 1)
                bias = vec[:, V_T1 + j:V_T1 + j + 1]
                act.activation(h1_split[:, 0, j, :], acc[j][:], ACT.Relu, bias=bias)
                act.activation(acc[j][:], acc[j][:], ACT.Relu, bias=bias).then_inc(h1_hi, 1)
            for j in range(D2 // P):
                act.wait_ge(mm_done, S_T2 + j + 1)
                act.activation(h2[:, j, :], acc[j][:], ACT.Relu,
                               bias=vec[:, V_T2 + j:V_T2 + j + 1]).then_inc(acc_free[j], 1)

        @block.vector
        def _(dve):
            links = [0]

            def link(ins):
                links[0] += 1
                ins.then_inc(prep, 1)
                dve.wait_ge(prep, links[0])

            def cols(ap, n, *shape):
                return ap.broadcast_to([P, *shape]) if n is None else ap

            dve.wait_ge(consts_set, 1)
            dve.wait_ge(ids_in, 32)
            dve.tensor_copy(fields_f[:], fields_i[:])
            link(dve.tensor_tensor(row_no[:], ids_sb[:], offs[:].unsqueeze(1).broadcast_to([P, BT, NF]), ALU.add))
            link(dve.tensor_tensor(onehot[:], fields_f[:].unsqueeze(2).broadcast_to([P, NSLOT, NF]),
                                   field_no[:].unsqueeze(1).broadcast_to([P, NSLOT, NF]), ALU.is_equal))
            dve.tensor_scalar(is_t0[:], fields_f[:], fields_f[:, 0:1], None, ALU.is_equal)
            dve.tensor_scalar(is_t1[:], fields_f[:], fields_f[:, 1:2], None, ALU.is_equal)
            link(dve.tensor_tensor(picked[:], onehot[:].unsqueeze(2).broadcast_to([P, NSLOT, BT, NF]),
                                   row_no[:].unsqueeze(1).broadcast_to([P, NSLOT, BT, NF]), ALU.mult))
            dve.tensor_reduce(slot_row[:], picked[:], AX.X, ALU.add)
            link(dve.tensor_tensor(skip[:], is_t0[:], is_t1[:], ALU.max))
            link(dve.memset(skip[:, 0:2], 0.0))
            link(dve.scalar_tensor_tensor(out=slot_row[:], in0=skip[:].unsqueeze(2).broadcast_to([P, NSLOT, BT]),
                                          scalar=float(V), in1=slot_row[:], op0=ALU.mult, op1=ALU.add))
            dve.tensor_scalar(slot_idx[:, :, 0, :], slot_row[:], 2.0, None, ALU.mult)
            dve.tensor_scalar(slot_idx[:, :, 1, :], slot_row[:], 2.0, 1.0, ALU.mult, ALU.add).then_inc(idx_set, 1)

            def lo_of_weights(r, rw, made):
                dve.wait_ge(w_hi, made)
                dve.tensor_tensor(w_split[:, r, 1, :], w_raw[:, rw, :], w_split[:, r, 0, :].bitcast(F32),
                                  ALU.subtract).then_inc(w_lo, 1)

            def chunk_lo(c):
                lo_of_weights(c % WR, c % RR, c + 1)

            def slot_chunk_lo(s, h):
                lo_of_weights((h + 3) % WR, (h + 3) % RR, s * KT + (C_PAIR + h + 4))

            for c in range(3):
                chunk_lo(c)

            dve.tensor_reduce(paired[:], onehot[:, 2:NSLOT, :].rearrange("p s f -> p f s"), AX.X, ALU.max)
            link(dve.tensor_tensor(notted[:], onehot[:, 0, :], onehot[:, 1, :], ALU.max))
            link(dve.tensor_scalar(remain[:], paired[:], -1.0, 1.0, ALU.mult, ALU.add))
            dve.tensor_reduce(n_rest[:], remain[:], AX.X, ALU.add)
            link(dve.tensor_tensor(w_row[:], remain[:], notted[:], ALU.is_gt))
            link(dve.tensor_scalar(rest_row[:].rearrange("p t f -> p f t"),
                                   w_row[:].unsqueeze(2).broadcast_to([P, NF, BT]), -float(V), float(V), ALU.mult, ALU.add))
            dve.tensor_tensor(rest_idx[:], rest_row[:], row_no[:], ALU.add).then_inc(idx_set, 1)
            dve.tensor_scalar(not_same[:], is_t0[:, 1:2], -1.0, 1.0, ALU.mult, ALU.add)
            link(dve.tensor_tensor(w_not[:], onehot[:, 0:2, :], remain[:].unsqueeze(1).broadcast_to([P, 2, NF]), ALU.mult))
            link(dve.tensor_reduce(w_t[:], w_not[:], AX.X, ALU.add))
            dve.tensor_scalar(w_t[:, 1:2], w_t[:, 1:2], not_same[:, 0:1], None, ALU.mult)
            link(dve.tensor_scalar(n_rest[:], n_rest[:], float(NPAIR), None, ALU.add))
            link(dve.reciprocal(inv_count[:], n_rest[:]))
            dve.wait_ge(vec_in, 16)
            link(dve.scalar_tensor_tensor(out=z_bias[:], in0=vec[:, V_A2:V_A2 + KT], scalar=2.0,
                                          in1=vec[:, V_O2:V_O2 + KT], op0=ALU.mult, op1=ALU.add))
            link(dve.tensor_scalar(z_bias[:], z_bias[:], inv_count[:, 0:1], None, ALU.mult))
            dve.tensor_copy(masks[:].rearrange("p (s m) -> p s m", m=2)[:, :, 0], is_t0[:])
            link(dve.tensor_copy(masks[:].rearrange("p (s m) -> p s m", m=2)[:, :, 1], is_t1[:]))

            def operand_lo(dst, h, made):
                bank = tps[h % TB][:].rearrange("p t b -> p (t b)")
                dve.wait_ge(op_hi, made)
                dve.tensor_tensor(dst[:, 1, h, :], bank, dst[:, 0, h, :].bitcast(F32), ALU.subtract)\
                    .then_inc(tr_free[h % TB], 1)

            for n in range(2 * KT):
                operand_lo(xs[n // KT], n % KT, n + 1)

            n = 0
            for g in range(16):
                u, f, j = g % 8, g % 4 // 2, g // 4 * 2 + g % 2
                if u in SPLIT_AT:
                    chunk_lo(g // 8 * 4 + SPLIT_AT[u])
                for _ in range(REST_AT[u]):
                    t, fld = divmod(n, NF)
                    add = rest_acc[:, t % 2, :]
                    if fld == 0 and t >= 2:
                        dve.wait_ge(tr_done, U_REST + 2 * (t - 1))
                    dve.wait_ge(rest_in[n % 2], 16 * (n // 2 + 1))
                    if fld == 0:
                        ins = dve.tensor_scalar(add, rest_ring[:, n % 2, :], w_row[:, fld:fld + 1], None, ALU.mult)
                    else:
                        dve.wait_ge(rest_summed, n)
                        ins = dve.scalar_tensor_tensor(out=add, in0=rest_ring[:, n % 2, :], scalar=w_row[:, fld:fld + 1],
                                                       in1=add, op0=ALU.mult, op1=ALU.add)
                    ins.then_inc(rest_summed, 1)
                    n += 1
                dve.wait_ge(hid_hi, g + 1)
                dve.tensor_tensor(us[f][:, 1, j, :], acc[g % MB][:], us[f][:, 0, j, :].bitcast(F32), ALU.subtract)\
                    .then_inc(acc_free[g % MB], 1)

            def pick(m, h, so_far):
                bank = tps[h % TB][:].rearrange("p t b -> p (t b)")
                dve.copy_predicated(bank, mask_now[:, m:m + 1].broadcast_to([P, B]), not_out[:, m, h, :])\
                    .then_inc((picked0, picked1)[m], 1)
                if m == 0:
                    dve.wait_ge(picked0, so_far)

            def set_masks(s):
                dve.tensor_copy(mask_now[:], masks[:, 2 * s + 4:2 * s + 6]).then_inc(mask_set, 1)
                dve.wait_ge(mask_set, s + 1)

            dve.wait_ge(tr_free[TB - 1], U_SLOT // TB)
            set_masks(0)
            for g in range(16):
                u, f, j = g % 8, g % 4 // 2, g // 4 * 2 + g % 2
                if u in SPLIT_AT:
                    chunk_lo(KT + g // 8 * 4 + SPLIT_AT[u])
                dve.wait_ge(acc_free[g % MB], (S_N2 + g) // MB + 1)
                if u in A0_AT:
                    h = g // 8 * 4 + A0_AT.index(u)
                    dve.wait_ge(tr_done, U_SLOT + h + 1)
                    pick(0, h, h + 1)
                    pick(1, h, h + 1)
                if f == 1:
                    dve.wait_ge(t_added, g - 1)
                dve.scalar_tensor_tensor(out=z_add[:, j, :], in0=not_out[:, f, j, :], scalar=w_t[:, f:f + 1],
                                         in1=z_add[:, j, :], op0=ALU.mult, op1=ALU.add).then_inc(t_added, 1)
                if u in A0_AT:
                    operand_lo(slot_split[0], h, 2 * KT + h + 1)

            def build(s, dst, h):
                dve.wait_ge(tr_done, s * KT + (U_SLOT + h + 1))
                pick(0, h, s * KT + (h + 1))
                pick(1, h, None)
                slot_chunk_lo(s - 1, h)
                operand_lo(dst, h, s * KT + (2 * KT + h + 1))

            def add_partial(s, h):
                dve.wait_ge(mm_done, s * KT + (S_PAIR + h + 1))
                dve.wait_ge(acc_free[h % MB], s * 2 + ((S_PAIR - KT + h) // MB + 1))
                dve.tensor_tensor(acc[h % MB][:], acc[h % MB][:], partial[:, h, :], ALU.add).then_inc(pair_in, 1)

            for i in range(2):
                set_masks(i * 2 + 1)
                for h in range(KT):
                    build(i * 2 + 1, slot_split[1], h)
                dve.wait_ge(sum_zeroed, 1)
                set_masks(i * 2 + 2)
                for h in range(KT):
                    build(i * 2 + 2, slot_split[0], h)
                    add_partial(i * 2 + 1, h)
                    dve.wait_ge(pair_in, i * KT + (h + 1))
                    dve.scalar_tensor_tensor(out=and_sum[:, h, :], in0=acc[h % MB][:], scalar=0.0,
                                             in1=and_sum[:, h, :], op0=ALU.max, op1=ALU.add)\
                        .then_inc(acc_free[h % MB], 1)
            set_masks(5)
            for h in range(KT):
                build(5, slot_split[1], h)
            for h in range(KT):
                if h < KT - 1:
                    slot_chunk_lo(5, h)
                dve.wait_ge(and_hi, h + 1)
                dve.tensor_tensor(and_split[:, 1, h, :], and_sum[:, h, :], and_split[:, 0, h, :].bitcast(F32),
                                  ALU.subtract).then_inc(and_lo, 1)
                dve.wait_ge(t_added, 2 * KT)
                dve.tensor_scalar(z_add[:, h, :], z_add[:, h, :], inv_count[:, 0:1], z_bias[:, h:h + 1],
                                  ALU.mult, ALU.add).then_inc(z_fin, 1)
                add_partial(5, h)
                dve.wait_ge(or_hi, h + 1)
                dve.scalar_tensor_tensor(out=or_split[:, 1, h, :], in0=acc[h % MB][:], scalar=0.0,
                                         in1=or_split[:, 0, h, :].bitcast(F32), op0=ALU.max, op1=ALU.subtract)\
                    .then_inc(acc_free[h % MB], 1)

            for j in range(KT):
                for c in (C_L2 + 2 + 2 * j, C_L2 + 3 + 2 * j):
                    chunk_lo(c)
                if j == 4:
                    dve.wait_ge(dense_hi, 1)
                    dve.tensor_tensor(dense_split[:, 1, :], dense_raw[:], dense_split[:, 0, :].bitcast(F32),
                                      ALU.subtract).then_inc(dense_lo, 1)
                dve.wait_ge(z_fin, j + 1)
                dve.wait_ge(mm_done, S_L2 + j + 1)
                dve.scalar_tensor_tensor(out=acc[j % MB][:], in0=acc[j % MB][:], scalar=inv_count[:, 0:1],
                                         in1=z_add[:, j, :], op0=ALU.mult, op1=ALU.add).then_inc(z_in, 1)
                dve.wait_ge(z_hi, j + 1)
                dve.tensor_tensor(z_split[:, 1, j, :], acc[j % MB][:], z_split[:, 0, j, :].bitcast(F32),
                                  ALU.subtract).then_inc(acc_free[j % MB], 1)
            for c in (C_T1 + 2, C_T1 + 3, C_T2):
                chunk_lo(c)
            for j in range(D1 // P):
                dve.wait_ge(h1_hi, j + 1)
                dve.tensor_tensor(h1_split[:, 1, j, :], acc[j][:], h1_split[:, 0, j, :].bitcast(F32),
                                  ALU.subtract).then_inc(acc_free[j], 1)
            dve.wait_ge(mm_done, S_T3 + 1)
            dve.tensor_copy(y[:], acc[2][0:1, :]).then_inc(y_set, 1)


def kernel(**inputs):
    import numpy as np
    import concourse.bacc as bacc
    from concourse.bass_utils import run_bass_kernel_spmd

    def chunked(w):
        k, n = w.shape
        return w.reshape(k // P, P, n // P, P).transpose(2, 1, 0, 3).reshape(n // P, P, k)

    def columns(v):
        return v.reshape(-1, P).T

    a = {n: np.asarray(v) for n, v in inputs.items()}
    tables = [a[f"tbl_{f}"] for f in range(NF)]
    sizes = [t.shape[0] for t in tables]
    offsets = [sum(sizes[:f]) for f in range(NF)]
    r = {n: a["L0_rec_" + n] for n in ("Wn1", "bn1", "Wn2", "bn2", "Wa1", "ba1", "Wa2", "ba2", "Wo1", "bo1", "Wo2", "bo2")}
    second = np.stack([chunked(r["Wa2"]), chunked(r["Wo2"])], axis=1).reshape(2 * KT, P, H)
    top2 = chunked(a["W_top2"])
    chunks = np.concatenate([
        chunked(r["Wn1"]), chunked(r["Wn2"]),
        chunked(r["Wa1"][:H]), chunked(r["Wa1"][H:]), chunked(r["Wo1"][:H]), chunked(r["Wo1"][H:]),
        second, chunked(a["W_top1"][:H]), top2.transpose(1, 0, 2).reshape(1, P, H)])
    vectors = np.concatenate([columns(v) for v in (
        r["bn1"], r["bn2"], r["ba1"], r["ba2"], r["bo1"], r["bo2"], a["b_top1"], a["b_top2"], a["W_top3"][:, 0])], axis=1)
    fields = np.concatenate([a["L0_rec_not_idx"], a["L0_rec_and_pairs"].reshape(-1), a["L0_rec_or_pairs"].reshape(-1)])

    arrays = {
        "table": np.concatenate(tables), "ids": a["ids"], "fields": fields, "chunks": chunks, "vectors": vectors,
        "dense": a["dense_ctx"].T, "w_dense": a["W_top1"][H:],
    }
    nc = bacc.Bacc("TRN2", target_bir_lowering=False, num_devices=1)
    arrays = {n: np.ascontiguousarray(v) for n, v in arrays.items()}
    args = [nc.dram_tensor(n, v.shape, mybir.dt.from_np(v.dtype), kind="ExternalInput").ap() for n, v in arrays.items()]
    out = nc.dram_tensor("out", (B, 1), F32, kind="ExternalOutput").ap()
    program(nc, *args, out, offsets)
    return run_bass_kernel_spmd(nc, [arrays], core_ids=[0]).results[0]["out"]
```

```python
from contextlib import ExitStack

import concourse.bass as bass
from concourse import mybir

ALU = mybir.AluOpType
ACT = mybir.ActivationFunctionType
AX = mybir.AxisListType
F32 = mybir.dt.float32
F32R = mybir.dt.float32r
I32 = mybir.dt.int32

P = 128
B = 512
H = 1024
KT = H // P
BT = B // P
NF = 8
NSLOT = 8
NPAIR = 3
HALF = H // 2
MB, TB = 4, 4
WR = 4
RR = 2
D1, D2 = 512, 256
KD = 16

S_N1, S_N2, S_PAIR, S_L2, S_T1, S_T2, S_T3 = 0, 16, 32, 80, 88, 92, 94
C_PAIR, C_L2, C_T1, C_T2 = 16, 64, 80, 84
N_CHUNK = 85
U_N1, U_REST, U_SLOT = 8, 16, 24
V_N1, V_N2, V_A1, V_A2, V_O1, V_O2, V_T1, V_T2, V_W3 = 0, 8, 16, 24, 32, 40, 48, 52, 54
NV = 56
SPLIT_AT = {0: 3, 3: 4, 4: 5, 7: 6}
A0_AT = (4, 5, 6, 7, 10, 11, 14, 15)
REST_AT = (0, 3, 3, 2)
REST_RING = 3
REST_TR = (5, 9, 13, 17)


def steps_of_not_chunk(c):
    layer, j = divmod(c, KT)
    return 16 * layer + j // 2 * 4 + j % 2 + 3


def program(nc, table, ids, fields, chunks, vectors, dense, w_dense, out, offsets):
    V = table.shape[0]
    chunk_rows = chunks.rearrange("c p n -> (c p) n")
    half_rows = table.rearrange("v (g c) -> (v g) c", g=2)

    with ExitStack() as ctx:
        base = (nc.sbuf_base + 63) // 64 * 64
        used = [base]

        def place(name, shape, dt, at=None):
            size = 4
            for n in shape[1:]:
                size *= n
            if at is None:
                at = used[0]
                used[0] += (size + 31) // 32 * 32
            return nc.alloc_sbuf_tensor_at(name, shape, dt, offset=at)

        SPLIT = 2 * KT * B * 4
        area = [used[0] + i * SPLIT for i in range(4)]
        used[0] += 4 * SPLIT
        at_a, at_b, at_c, at_d = area
        xs = [place("x0_split", [P, 2, KT, B], F32R, at_a), place("x1_split", [P, 2, KT, B], F32R, at_b)]
        us = [place("u0_split", [P, 2, KT, B], F32R, at_c), place("u1_split", [P, 2, KT, B], F32R, at_d)]
        not_out = place("not_out", [P, 2, KT, B], F32, at_a)
        slot_split = [place("slot_even", [P, 2, KT, B], F32R, at_b), place("slot_odd", [P, 2, KT, B], F32R, at_c)]
        or_split = place("or_split", [P, 2, KT, B], F32R, at_a)
        and_split = place("and_split", [P, 2, KT, B], F32R, at_b)
        z_split = place("z_split", [P, 2, KT, B], F32R, at_c)
        rows1 = place("rows_input1", [P, BT, H], F32, at_d)
        partial = place("partial", [P, KT, B], F32, at_d)
        and_sum = place("and_sum", [P, KT, B], F32, at_d + SPLIT // 2)
        h1_split = place("h1_split", [P, 2, D1 // P, B], F32R, at_d)
        h2 = place("h2", [P, D2 // P, B], F32, at_d + SPLIT // 2)
        y = place("y", [1, B], F32, at_d + SPLIT // 2 + D2 // P * B * 4)
        at_rows = used[0]
        rows = place("rows", [P, 2, BT, HALF], F32)
        rest_ring = place("rest_ring", [P, REST_RING, H], F32, at_rows)
        rest_acc = place("rest_acc", [P, H], F32, at_rows + REST_RING * H * 4)
        dense_raw = place("dense_raw", [KD, B + D1], F32, at_rows)
        dense_split = place("dense_split", [KD, 2, B + D1], F32R, at_rows + (B + D1) * 4)
        z_add = place("z_add", [P, KT, B], F32)
        w_raw = place("w_raw", [P, RR, KT * P], F32)
        w_split = place("w_split", [P, WR, 2, KT * P], F32R)
        ident = place("ident", [P, P], F32)
        vec = place("vec", [P, NV], F32)
        z_bias = place("z_bias", [P, KT], F32)
        ids_sb = place("ids_sb", [P, BT, NF], I32)
        fields_i = place("fields_i", [P, NSLOT], I32)
        fields_f = place("fields_f", [P, NSLOT], F32)
        field_no = place("field_no", [P, NF], F32)
        offs = place("offs", [P, NF], F32)
        row_no = place("row_no", [P, BT, NF], F32)
        onehot = place("onehot", [P, NSLOT, NF], F32)
        picked = place("picked", [P, NSLOT, BT, NF], F32)
        slot_row = place("slot_row", [P, NSLOT, BT], F32)
        row1_idx = place("row1_idx", [P, BT], I32)
        slot_idx = place("slot_idx", [P, NSLOT, 2, BT], I32)
        is_t0 = place("is_t0", [P, NSLOT], F32)
        is_t1 = place("is_t1", [P, NSLOT], F32)
        skip = place("skip", [P, NSLOT], F32)
        masks = place("masks", [P, NSLOT * 2], I32)
        mask_now = place("mask_now", [P, 2], I32)
        paired = place("paired", [P, NF], F32)
        notted = place("notted", [P, NF], F32)
        remain = place("remain", [P, NF], F32)
        w_row = place("w_row", [P, NF], F32)
        rest_row = place("rest_row", [P, BT, NF], F32)
        rest_idx = place("rest_idx", [P, BT, NF], I32)
        w_not = place("w_not", [P, 2, NF], F32)
        w_t = place("w_t", [P, 2], F32)
        not_same = place("not_same", [P, 1], F32)
        n_rest = place("n_rest", [P, 1], F32)
        inv_count = place("inv_count", [P, 1], F32)
        nc.sbuf_tensor("fence", [P, used[0] - nc.sbuf_base], mybir.dt.uint8).__enter__()

        acc = [ctx.enter_context(nc.psum_tensor(f"acc{i}", [P, B], F32)) for i in range(MB)]
        tps = [ctx.enter_context(nc.psum_tensor(f"tps{i}", [P, BT, P], F32)) for i in range(TB)]

        def sem(name):
            return ctx.enter_context(nc.semaphore(name))

        ids_in = sem("ids_in")
        vec_in = sem("vec_in")
        dense_in = sem("dense_in")
        raw_in = [sem(f"raw_in{i}") for i in range(RR)]
        w_hi = sem("w_hi")
        w_lo = sem("w_lo")
        consts_set = sem("consts_set")
        prep = sem("prep")
        idx_set = sem("idx_set")
        rows_in = [sem(f"rows_in{g}") for g in range(2)]
        rows1_in = sem("rows1_in")
        rest_in = [sem(f"rest_in{r}") for r in range(REST_RING)]
        rest_summed = sem("rest_summed")
        tr_done = sem("tr_done")
        tr_free = [sem(f"tr_free{i}") for i in range(TB)]
        picked0 = sem("picked0")
        picked1 = sem("picked1")
        op_hi = sem("op_hi")
        mm_done = sem("mm_done")
        acc_free = [sem(f"acc_free{i}") for i in range(MB)]
        hid_hi = sem("hid_hi")
        t_added = sem("t_added")
        mask_set = sem("mask_set")
        pair_in = sem("pair_in")
        and_hi = sem("and_hi")
        and_lo = sem("and_lo")
        or_hi = sem("or_hi")
        z_fin = sem("z_fin")
        z_in = sem("z_in")
        z_hi = sem("z_hi")
        dense_hi = sem("dense_hi")
        dense_lo = sem("dense_lo")
        h1_hi = sem("h1_hi")
        y_set = sem("y_set")
        stored = sem("stored")

        block = ctx.enter_context(nc.Block())

        @block.sync
        def _(sp):
            sp.dma_start(ids_sb[:], ids.rearrange("(t p) f -> p t f", p=P)).then_inc(ids_in, 16)
            sp.dma_start(fields_i[:], fields.partition_broadcast(P)).then_inc(ids_in, 16)

            def load(chunk, c, r, first=False):
                if not first:
                    sp.wait_ge(w_lo, c - 1)
                sp.dma_start(w_raw[:, r, :], chunk_rows[bass.ds(chunk * P, P), :]).then_inc(raw_in[r], 16)

            load(0, 0, 0, first=True)
            load(1, 1, 1, first=True)
            sp.dma_start(vec[:], vectors).then_inc(vec_in, 16)
            with sp.Fori(1, 16) as i:
                for r in range(RR):
                    load(i * 2 + r, i * 2 + r, r)
            with sp.Fori(16, 40) as i:
                for r in range(RR):
                    load(i * 2 + (r - 16), i * 2 + r, r)
            for c in range(80, N_CHUNK):
                load(c - 16, c, c % RR)
            sp.wait_ge(y_set, 1)
            sp.dma_start(out.rearrange("b o -> o b"), y[:]).then_inc(stored, 16)
            sp.wait_ge(stored, 16)

        @block.gpsimd
        def _(pool):
            for f in range(NF):
                pool.memset(offs[:, f:f + 1], float(offsets[f]))
                pool.memset(field_no[:, f:f + 1], float(f))
            pool.memset(ident[:], 0.0).then_inc(consts_set, 1)
            pool.wait_ge(consts_set, 1)
            pool.affine_select(out=ident[:], in_=ident[:], compare_op=ALU.not_equal, fill=1.0, base=0,
                               pattern=[[-1, P]], channel_multiplier=1).then_inc(consts_set, 1)

            def gather(dst, src, idx, landed):
                pool.indirect_dma_start(dst, None, src, bass.IndirectOffsetOnAxis(ap=idx, axis=0),
                                        bounds_check=src.shape[0] - 1, oob_is_err=False).then_inc(landed, 16)

            pool.wait_ge(idx_set, 1)
            for g in range(2):
                for t in range(BT):
                    gather(rows[:, g, t, :], half_rows, slot_idx[:, 0, g, t:t + 1], rows_in[g])
            for t in range(BT):
                gather(rows1[:, t, :], table, row1_idx[:, t:t + 1], rows1_in)
            pool.wait_ge(idx_set, 2)
            pool.wait_ge(tr_done, KT)
            for n in range(BT * NF):
                r = n % REST_RING
                if n >= REST_RING:
                    pool.wait_ge(rest_summed, n - REST_RING + 1)
                gather(rest_ring[:, r, :], table, rest_idx[:, n // NF, n % NF:n % NF + 1], rest_in[r])
            pool.wait_ge(idx_set, 3)
            pool.wait_ge(tr_done, U_SLOT)

            for s in range(2 * NPAIR):
                for g in range(2):
                    if s >= 1:
                        pool.wait_ge(tr_done, U_SLOT + (s - 1) * KT + 4 * (g + 1))
                    for t in range(BT):
                        gather(rows[:, g, t, :], half_rows, slot_idx[:, 2 + s, g, t:t + 1], rows_in[g])

            pool.wait_ge(tr_done, U_SLOT + 6 * KT)
            pool.dma_start(dense_raw[:, 0:B], dense).then_inc(dense_in, 16)
            pool.dma_start(dense_raw[:, B:B + D1], w_dense).then_inc(dense_in, 16)

        @block.tensor
        def _(pe):
            def unit(src, bank, h):
                for t in range(BT):
                    c = h % 4 * P
                    ins = pe.transpose(tps[bank][:, t, :], src[:, h // 4, t, c:c + P], ident[:])
                ins.then_inc(tr_done, 1)

            def slot_unit(s, h, bank):
                if bank == 0:
                    pe.wait_ge(rows_in[h // 4], s * 64 + 128)
                pe.wait_ge(tr_free[bank], s * 2 + (U_SLOT + h) // 4)
                unit(rows, bank, h)

            def product(bank, w, x, k, wk, start, stop):
                lhs = [w_split[:, w, p, wk * P:(wk + 1) * P] for p in range(2)]
                for n, (a, b) in enumerate(((0, 0), (1, 0), (0, 1))):
                    ins = pe.matmul(acc[bank][:], lhs[a], x[:, b, k, :], start=start and n == 0, stop=stop and n == 2)
                return ins

            def input_units(ns):
                for n in ns:
                    if n >= TB:
                        pe.wait_ge(tr_free[n % TB], n // TB)
                    for t in range(BT):
                        src = rows[:, n // 4, t, n % 4 * P:(n % 4 + 1) * P] if n < KT else rows1[:, t, (n - KT) * P:(n - KT + 1) * P]
                        ins = pe.transpose(tps[n % TB][:, t, :], src, ident[:])
                    ins.then_inc(tr_done, 1)

            def rest_units(t):
                pe.wait_ge(rest_summed, NF * (t + 1))
                for q in range(2):
                    n = U_REST + 2 * t + q
                    pe.wait_ge(tr_free[n % TB], n // TB)
                    for h in range(4):
                        ins = pe.transpose(tps[n % TB][:, h, :], rest_acc[:, (4 * q + h) * P:(4 * q + h + 1) * P], ident[:])
                    ins.then_inc(tr_done, 1)

            pe.wait_ge(consts_set, 2)
            pe.wait_ge(rows_in[0], 64)
            input_units(range(0, 4))
            for k in range(KT):
                if k == 2:
                    pe.wait_ge(rows_in[1], 64)
                    input_units(range(4, 8))
                if k == 6:
                    pe.wait_ge(rows1_in, 64)
                    input_units(range(8, 12))
                pe.wait_ge(tr_free[k % TB], k // TB + 1)
                for g in range(2):
                    if k == 0:
                        pe.wait_ge(w_lo, g + 1)
                    ins = product(g, g, xs[0], k, k, k == 0, k == KT - 1)
                    if k == KT - 1:
                        ins.then_inc(mm_done, 1)
            input_units(range(12, 16))
            for g in range(2, 16):
                f, c = g % 4 // 2, g % 8 // 4 * 2 + g % 2
                if g in REST_TR:
                    rest_units(REST_TR.index(g))
                pe.wait_ge(w_lo, g // 8 * 4 + c + 1)
                if g >= MB:
                    pe.wait_ge(acc_free[g % MB], g // MB)
                for k in range(KT):
                    if g == 2:
                        pe.wait_ge(tr_free[k % TB], (KT + k) // TB + 1)
                    ins = product(g % MB, c, xs[f], k, k, k == 0, k == KT - 1)
                ins.then_inc(mm_done, 1)

            for g in range(16):
                u, f, c = g % 8, g % 4 // 2, g % 8 // 4 * 2 + g % 2
                if S_N2 + g in REST_TR:
                    rest_units(REST_TR.index(S_N2 + g))
                if g in A0_AT:
                    slot_unit(0, A0_AT.index(g), A0_AT.index(g) % TB)
                pe.wait_ge(acc_free[1 + 2 * f], 4)
                pe.wait_ge(w_lo, KT + g // 8 * 4 + c + 1)
                pe.wait_ge(acc_free[u % MB], (S_N2 + g) // MB)
                for k in range(KT):
                    ins = product(u % MB, c, us[f], k, k, k == 0, k == KT - 1)
                ins.then_inc(mm_done, 1)

            def slot_steps(s, par, build):
                for h in range(KT):
                    if build:
                        slot_unit(s + 1, h, h % 4)
                    pe.wait_ge(w_lo, s * KT + (C_PAIR + h + 1))
                    pe.wait_ge(acc_free[h % 4], s * 2 + (S_PAIR + h) // 4)
                    for k in range(KT):
                        if h == 0 and k in (0, 6, 7):
                            n = U_SLOT + max(k, 5)
                            pe.wait_ge(tr_free[n % TB], s * 2 + (n // TB + 1))
                        ins = product(h % 4, h % 4, slot_split[par], k, k, k == 0, k == KT - 1)
                    ins.then_inc(mm_done, 1)

            with pe.Fori(0, 2) as i:
                slot_steps(i * 2, 0, True)
                slot_steps(i * 2 + 1, 1, True)
            slot_steps(4, 0, True)
            slot_steps(5, 1, False)

            with pe.Fori(0, 2) as hh:
                for u in range(4):
                    pe.wait_ge(acc_free[u], hh + S_L2 // 4)
                    for part, x in enumerate((and_split, or_split)):
                        w = 2 * u + part
                        pe.wait_ge(w_lo, hh * 8 + (C_L2 + w + 1))
                        for k in range(KT):
                            if part == 0 and k == 0:
                                pe.wait_ge(and_lo, KT)
                            if part == 1 and k in (0, KT - 1):
                                pe.wait_ge(acc_free[2 + k // (KT - 1)], S_L2 // MB)
                            ins = product(u, w % 4, x, k, k, part + k == 0, part == 1 and k == KT - 1)
                    ins.then_inc(mm_done, 1)

            for j in range(D1 // P):
                pe.wait_ge(w_lo, C_T1 + j + 1)
                pe.wait_ge(acc_free[j], (S_T1 + j) // 4)
                pe.wait_ge(acc_free[2], S_T1 // MB)
                for k in range(KT - 1):
                    product(j, j, z_split, k, k, k == 0, False)
            pe.wait_ge(dense_lo, 1)
            pe.wait_ge(acc_free[3], S_T1 // MB)
            for j in range(D1 // P):
                product(j, j, z_split, KT - 1, KT - 1, False, False)
                for n, (a, b) in enumerate(((0, 0), (1, 0), (0, 1))):
                    ins = pe.matmul(acc[j][:], dense_split[:, a, B + j * P:B + (j + 1) * P], dense_split[:, b, 0:B],
                                    start=False, stop=n == 2)
                ins.then_inc(mm_done, 1)

            K2 = D1 // P
            pe.wait_ge(w_lo, C_T2 + 1)
            for k in range(K2):
                pe.wait_ge(acc_free[k], S_T2 // MB)
                if k == 0:
                    pe.wait_ge(acc_free[1], S_T2 // MB)
                for j in range(D2 // P):
                    ins = product(j, C_T2 % WR, h1_split, k, j * K2 + k, k == 0, k == K2 - 1)
                    if k == K2 - 1:
                        ins.then_inc(mm_done, 1)

            pe.wait_ge(vec_in, 16)
            pe.wait_ge(acc_free[2], (S_T3) // 4)
            for k in range(D2 // P):
                pe.wait_ge(acc_free[k], S_T2 // MB + 1)
                ins = pe.matmul(acc[2][0:1, :], vec[:, V_W3 + k:V_W3 + k + 1], h2[:, k, :], start=k == 0, stop=k == D2 // P - 1)
            ins.then_inc(mm_done, 1)

        @block.scalar
        def _(act):
            def weights_hi(r, rw, landed, steps=None):
                act.wait_ge(raw_in[rw], landed)
                if steps is not None:
                    act.wait_ge(mm_done, steps)
                act.copy(w_split[:, r, 0, :], w_raw[:, rw, :]).then_inc(w_hi, 1)

            def chunk_hi(c, steps=None):
                weights_hi(c % WR, c % RR, 16 * (c // RR + 1), steps)

            def slot_chunk_hi(s, h):
                weights_hi((h + 3) % WR, (h + 3) % RR, s * 64 + 16 * ((C_PAIR + h + 3) // RR + 1),
                           s * KT + (S_PAIR + h))

            def operand_hi(dst, h):
                act.copy(dst[:, 0, h, :], tps[h % TB][:].rearrange("p t b -> p (t b)")).then_inc(op_hi, 1)

            for c in range(2):
                chunk_hi(c)
            for n in range(2 * KT):
                act.wait_ge(tr_done, n + 1)
                operand_hi(xs[n // KT], n % KT)
                if n == KT - 1:
                    chunk_hi(2)
                    chunk_hi(3)
            act.wait_ge(vec_in, 16)

            def move_rest(t):
                for q in range(2):
                    n = U_REST + 2 * t + q
                    act.wait_ge(tr_done, n + 1)
                    act.copy(z_add[:, 4 * q:4 * q + 4, t * P:(t + 1) * P], tps[n % TB][:]).then_inc(tr_free[n % TB], 1)

            for g in range(16):
                u, f, j = g % 8, g % 4 // 2, g // 4 * 2 + g % 2
                if u in SPLIT_AT and g > 0:
                    c = g // 8 * 4 + SPLIT_AT[u]
                    chunk_hi(c, steps_of_not_chunk(c - WR))
                if g in REST_TR:
                    move_rest(REST_TR.index(g))
                act.wait_ge(mm_done, g + 1)
                bias = vec[:, V_N1 + j:V_N1 + j + 1]
                act.activation(us[f][:, 0, j, :], acc[g % MB][:], ACT.Relu, bias=bias)
                act.activation(acc[g % MB][:], acc[g % MB][:], ACT.Relu, bias=bias).then_inc(hid_hi, 1)

            for g in range(16):
                u, f, j = g % 8, g % 4 // 2, g // 4 * 2 + g % 2
                if u in SPLIT_AT:
                    c = KT + g // 8 * 4 + SPLIT_AT[u]
                    chunk_hi(c, steps_of_not_chunk(c - WR))
                if S_N2 + g in REST_TR:
                    move_rest(REST_TR.index(S_N2 + g))
                act.wait_ge(mm_done, S_N2 + g + 1)
                act.activation(not_out[:, f, j, :], acc[g % MB][:], ACT.Tanh,
                               bias=vec[:, V_N2 + j:V_N2 + j + 1]).then_inc(acc_free[g % MB], 1)
                if g in A0_AT:
                    h = A0_AT.index(g)
                    act.wait_ge(picked1, h + 1)
                    operand_hi(slot_split[0], h)

            def first_operand(s, bias_at):
                for h in range(KT):
                    slot_chunk_hi(s, h)
                    act.wait_ge(picked1, s * KT + (KT + h + 1))
                    operand_hi(slot_split[1], h)
                    act.wait_ge(mm_done, s * KT + (S_PAIR + h + 1))
                    act.activation(partial[:, h, :], acc[h % MB][:], ACT.Identity,
                                   bias=vec[:, bias_at + h:bias_at + h + 1]).then_inc(acc_free[h % MB], 1)

            for i in range(2):
                first_operand(i * 2, V_A1)
                for h in range(KT):
                    slot_chunk_hi(i * 2 + 1, h)
                    act.wait_ge(picked1, i * (2 * KT) + (2 * KT + h + 1))
                    operand_hi(slot_split[0], h)
                    if i == 0:
                        act.wait_ge(pair_in, h + 1)
                        act.activation(and_sum[:, h, :], acc[h % MB][:], ACT.Relu).then_inc(acc_free[h % MB], 1)
            first_operand(4, V_O1)
            act.wait_ge(mm_done, S_PAIR + 5 * KT)
            act.wait_ge(acc_free[MB - 1], (S_PAIR + 4 * KT) // MB)
            for h in range(KT):
                if h < KT - 1:
                    slot_chunk_hi(5, h)
                act.copy(and_split[:, 0, h, :], and_sum[:, h, :]).then_inc(and_hi, 1)
                act.wait_ge(pair_in, 2 * KT + h + 1)
                act.activation(or_split[:, 0, h, :], acc[h % MB][:], ACT.Relu).then_inc(or_hi, 1)

            for j in range(KT):
                for c in (C_L2 + 2 + 2 * j, C_L2 + 3 + 2 * j):
                    chunk_hi(c, S_L2 + j)
                if j == 4:
                    act.wait_ge(dense_in, 32)
                    act.copy(dense_split[:, 0, :], dense_raw[:]).then_inc(dense_hi, 1)
                act.wait_ge(z_in, j + 1)
                act.copy(z_split[:, 0, j, :], acc[j % MB][:]).then_inc(z_hi, 1)
            for c in (C_T1 + 2, C_T1 + 3):
                chunk_hi(c, S_T1)
            chunk_hi(C_T2, S_T1 + 1)
            for j in range(D1 // P):
                act.wait_ge(mm_done, S_T1 + j + 1)
                bias = vec[:, V_T1 + j:V_T1 + j + 1]
                act.activation(h1_split[:, 0, j, :], acc[j][:], ACT.Relu, bias=bias)
                act.activation(acc[j][:], acc[j][:], ACT.Relu, bias=bias).then_inc(h1_hi, 1)
            for j in range(D2 // P):
                act.wait_ge(mm_done, S_T2 + j + 1)
                act.activation(h2[:, j, :], acc[j][:], ACT.Relu,
                               bias=vec[:, V_T2 + j:V_T2 + j + 1]).then_inc(acc_free[j], 1)

        @block.vector
        def _(dve):
            links = [0]

            def link(ins):
                links[0] += 1
                ins.then_inc(prep, 1)
                dve.wait_ge(prep, links[0])

            def cols(ap, n, *shape):
                return ap.broadcast_to([P, *shape]) if n is None else ap

            dve.wait_ge(consts_set, 1)
            dve.wait_ge(ids_in, 32)
            dve.tensor_copy(fields_f[:], fields_i[:])
            link(dve.tensor_tensor(row_no[:], ids_sb[:], offs[:].unsqueeze(1).broadcast_to([P, BT, NF]), ALU.add))
            link(dve.tensor_tensor(onehot[:], fields_f[:].unsqueeze(2).broadcast_to([P, NSLOT, NF]),
                                   field_no[:].unsqueeze(1).broadcast_to([P, NSLOT, NF]), ALU.is_equal))
            first = slice(0, 2)
            link(dve.tensor_tensor(picked[:, first], onehot[:, first].unsqueeze(2).broadcast_to([P, 2, BT, NF]),
                                   row_no[:].unsqueeze(1).broadcast_to([P, 2, BT, NF]), ALU.mult))
            link(dve.tensor_reduce(slot_row[:, first], picked[:, first], AX.X, ALU.add))
            dve.tensor_scalar(slot_idx[:, 0, 0, :], slot_row[:, 0, :], 2.0, None, ALU.mult)
            dve.tensor_scalar(slot_idx[:, 0, 1, :], slot_row[:, 0, :], 2.0, 1.0, ALU.mult, ALU.add)
            dve.tensor_copy(row1_idx[:], slot_row[:, 1, :]).then_inc(idx_set, 1)

            def lo_of_weights(r, rw, made):
                dve.wait_ge(w_hi, made)
                dve.tensor_tensor(w_split[:, r, 1, :], w_raw[:, rw, :], w_split[:, r, 0, :].bitcast(F32),
                                  ALU.subtract).then_inc(w_lo, 1)

            def chunk_lo(c):
                lo_of_weights(c % WR, c % RR, c + 1)

            def slot_chunk_lo(s, h):
                lo_of_weights((h + 3) % WR, (h + 3) % RR, s * KT + (C_PAIR + h + 4))

            for c in range(2):
                chunk_lo(c)

            dve.tensor_reduce(paired[:], onehot[:, 2:NSLOT, :].rearrange("p s f -> p f s"), AX.X, ALU.max)
            link(dve.tensor_tensor(notted[:], onehot[:, 0, :], onehot[:, 1, :], ALU.max))
            link(dve.tensor_scalar(remain[:], paired[:], -1.0, 1.0, ALU.mult, ALU.add))
            link(dve.tensor_tensor(w_row[:], remain[:], notted[:], ALU.is_gt))
            link(dve.tensor_scalar(rest_row[:].rearrange("p t f -> p f t"),
                                   w_row[:].unsqueeze(2).broadcast_to([P, NF, BT]), -float(V), float(V), ALU.mult, ALU.add))
            dve.tensor_tensor(rest_idx[:], rest_row[:], row_no[:], ALU.add).then_inc(idx_set, 1)

            def operand_lo(dst, h, made):
                bank = tps[h % TB][:].rearrange("p t b -> p (t b)")
                dve.wait_ge(op_hi, made)
                dve.tensor_tensor(dst[:, 1, h, :], bank, dst[:, 0, h, :].bitcast(F32), ALU.subtract)\
                    .then_inc(tr_free[h % TB], 1)

            for n in range(2 * KT):
                operand_lo(xs[n // KT], n % KT, n + 1)
                if n == KT - 1:
                    chunk_lo(2)
                    chunk_lo(3)

            dve.tensor_scalar(is_t0[:], fields_f[:], fields_f[:, 0:1], None, ALU.is_equal)
            dve.tensor_scalar(is_t1[:], fields_f[:], fields_f[:, 1:2], None, ALU.is_equal)
            link(dve.tensor_tensor(picked[:], onehot[:].unsqueeze(2).broadcast_to([P, NSLOT, BT, NF]),
                                   row_no[:].unsqueeze(1).broadcast_to([P, NSLOT, BT, NF]), ALU.mult))
            dve.tensor_reduce(slot_row[:], picked[:], AX.X, ALU.add)
            link(dve.tensor_tensor(skip[:], is_t0[:], is_t1[:], ALU.max))
            link(dve.scalar_tensor_tensor(out=slot_row[:], in0=skip[:].unsqueeze(2).broadcast_to([P, NSLOT, BT]),
                                          scalar=float(V), in1=slot_row[:], op0=ALU.mult, op1=ALU.add))
            dve.tensor_scalar(slot_idx[:, 2:, 0, :], slot_row[:, 2:], 2.0, None, ALU.mult)
            dve.tensor_scalar(slot_idx[:, 2:, 1, :], slot_row[:, 2:], 2.0, 1.0, ALU.mult, ALU.add).then_inc(idx_set, 1)

            dve.tensor_reduce(n_rest[:], remain[:], AX.X, ALU.add)
            dve.tensor_scalar(not_same[:], is_t0[:, 1:2], -1.0, 1.0, ALU.mult, ALU.add)
            link(dve.tensor_tensor(w_not[:], onehot[:, 0:2, :], remain[:].unsqueeze(1).broadcast_to([P, 2, NF]), ALU.mult))
            link(dve.tensor_reduce(w_t[:], w_not[:], AX.X, ALU.add))
            dve.tensor_scalar(w_t[:, 1:2], w_t[:, 1:2], not_same[:, 0:1], None, ALU.mult)
            link(dve.tensor_scalar(n_rest[:], n_rest[:], float(NPAIR), None, ALU.add))
            link(dve.reciprocal(inv_count[:], n_rest[:]))
            dve.wait_ge(vec_in, 16)
            link(dve.scalar_tensor_tensor(out=z_bias[:], in0=vec[:, V_A2:V_A2 + KT], scalar=2.0,
                                          in1=vec[:, V_O2:V_O2 + KT], op0=ALU.mult, op1=ALU.add))
            link(dve.tensor_scalar(z_bias[:], z_bias[:], inv_count[:, 0:1], None, ALU.mult))
            dve.tensor_copy(masks[:].rearrange("p (s m) -> p s m", m=2)[:, :, 0], is_t0[:])
            link(dve.tensor_copy(masks[:].rearrange("p (s m) -> p s m", m=2)[:, :, 1], is_t1[:]))

            n = 0
            for g in range(16):
                u, f, j = g % 8, g % 4 // 2, g // 4 * 2 + g % 2
                if u in SPLIT_AT and g > 0:
                    chunk_lo(g // 8 * 4 + SPLIT_AT[u])
                for _ in range(REST_AT[g % 4]):
                    t, fld = divmod(n, NF)
                    row, w = rest_ring[:, n % REST_RING, :], w_row[:, fld:fld + 1]
                    dve.wait_ge(rest_in[n % REST_RING], 16 * (n // REST_RING + 1))
                    if fld == 0:
                        if t >= 1:
                            dve.wait_ge(tr_done, U_REST + 2 * t)
                        ins = dve.tensor_scalar(rest_acc[:], row, w, None, ALU.mult)
                    else:
                        dve.wait_ge(rest_summed, n)
                        ins = dve.scalar_tensor_tensor(out=rest_acc[:], in0=row, scalar=w, in1=rest_acc[:],
                                                       op0=ALU.mult, op1=ALU.add)
                    ins.then_inc(rest_summed, 1)
                    n += 1
                dve.wait_ge(hid_hi, g + 1)
                dve.tensor_tensor(us[f][:, 1, j, :], acc[g % MB][:], us[f][:, 0, j, :].bitcast(F32), ALU.subtract)\
                    .then_inc(acc_free[g % MB], 1)

            def pick(m, h, so_far):
                bank = tps[h % TB][:].rearrange("p t b -> p (t b)")
                dve.copy_predicated(bank, mask_now[:, m:m + 1].broadcast_to([P, B]), not_out[:, m, h, :])\
                    .then_inc((picked0, picked1)[m], 1)
                if m == 0:
                    dve.wait_ge(picked0, so_far)

            def set_masks(s):
                dve.tensor_copy(mask_now[:], masks[:, 2 * s + 4:2 * s + 6]).then_inc(mask_set, 1)
                dve.wait_ge(mask_set, s + 1)

            set_masks(0)
            for g in range(16):
                if g % 8 in SPLIT_AT:
                    chunk_lo(KT + g // 8 * 4 + SPLIT_AT[g % 8])
                if g in A0_AT:
                    h = A0_AT.index(g)
                    dve.wait_ge(tr_done, U_SLOT + h + 1)
                    last = S_N2 + h // 2 * 4 + 2 + h % 2
                    dve.wait_ge(acc_free[last % MB], last // MB + 1)
                    pick(0, h, h + 1)
                    pick(1, h, h + 1)
                    operand_lo(slot_split[0], h, 2 * KT + h + 1)

            def add_not_result(f, j):
                if j == 0:
                    dve.wait_ge(tr_free[TB - 1], U_SLOT // TB)
                    if f == 1:
                        dve.wait_ge(t_added, KT)
                dve.scalar_tensor_tensor(out=z_add[:, j, :], in0=not_out[:, f, j, :], scalar=w_t[:, f:f + 1],
                                         in1=z_add[:, j, :], op0=ALU.mult, op1=ALU.add).then_inc(t_added, 1)

            def build(s, dst, h):
                dve.wait_ge(tr_done, s * KT + (U_SLOT + h + 1))
                pick(0, h, s * KT + (h + 1))
                pick(1, h, None)
                slot_chunk_lo(s - 1, h)
                operand_lo(dst, h, s * KT + (2 * KT + h + 1))

            def add_partial(s, h):
                dve.wait_ge(mm_done, s * KT + (S_PAIR + h + 1))
                dve.wait_ge(acc_free[h % MB], s * 2 + ((S_PAIR - KT + h) // MB + 1))
                dve.tensor_tensor(acc[h % MB][:], acc[h % MB][:], partial[:, h, :], ALU.add).then_inc(pair_in, 1)

            for i in range(2):
                set_masks(i * 2 + 1)
                for h in range(KT):
                    build(i * 2 + 1, slot_split[1], h)
                    add_not_result(i, h)
                set_masks(i * 2 + 2)
                for h in range(KT):
                    build(i * 2 + 2, slot_split[0], h)
                    add_partial(i * 2 + 1, h)
                    if i == 1:
                        dve.wait_ge(acc_free[h % MB], (S_PAIR + KT + h) // MB + 1)
                        dve.wait_ge(pair_in, KT + h + 1)
                        dve.scalar_tensor_tensor(out=and_sum[:, h, :], in0=acc[h % MB][:], scalar=0.0,
                                                 in1=and_sum[:, h, :], op0=ALU.max, op1=ALU.add)\
                            .then_inc(acc_free[h % MB], 1)
            set_masks(5)
            for h in range(KT):
                build(5, slot_split[1], h)
            for h in range(KT):
                if h < KT - 1:
                    slot_chunk_lo(5, h)
                dve.wait_ge(and_hi, h + 1)
                dve.tensor_tensor(and_split[:, 1, h, :], and_sum[:, h, :], and_split[:, 0, h, :].bitcast(F32),
                                  ALU.subtract).then_inc(and_lo, 1)
                dve.wait_ge(t_added, 2 * KT)
                dve.tensor_scalar(z_add[:, h, :], z_add[:, h, :], inv_count[:, 0:1], z_bias[:, h:h + 1],
                                  ALU.mult, ALU.add).then_inc(z_fin, 1)
                add_partial(5, h)
                dve.wait_ge(or_hi, h + 1)
                dve.scalar_tensor_tensor(out=or_split[:, 1, h, :], in0=acc[h % MB][:], scalar=0.0,
                                         in1=or_split[:, 0, h, :].bitcast(F32), op0=ALU.max, op1=ALU.subtract)\
                    .then_inc(acc_free[h % MB], 1)

            for j in range(KT):
                for c in (C_L2 + 2 + 2 * j, C_L2 + 3 + 2 * j):
                    chunk_lo(c)
                if j == 4:
                    dve.wait_ge(dense_hi, 1)
                    dve.tensor_tensor(dense_split[:, 1, :], dense_raw[:], dense_split[:, 0, :].bitcast(F32),
                                      ALU.subtract).then_inc(dense_lo, 1)
                dve.wait_ge(z_fin, j + 1)
                dve.wait_ge(mm_done, S_L2 + j + 1)
                dve.scalar_tensor_tensor(out=acc[j % MB][:], in0=acc[j % MB][:], scalar=inv_count[:, 0:1],
                                         in1=z_add[:, j, :], op0=ALU.mult, op1=ALU.add).then_inc(z_in, 1)
                dve.wait_ge(z_hi, j + 1)
                dve.tensor_tensor(z_split[:, 1, j, :], acc[j % MB][:], z_split[:, 0, j, :].bitcast(F32),
                                  ALU.subtract).then_inc(acc_free[j % MB], 1)
            for c in (C_T1 + 2, C_T1 + 3, C_T2):
                chunk_lo(c)
            for j in range(D1 // P):
                dve.wait_ge(h1_hi, j + 1)
                dve.tensor_tensor(h1_split[:, 1, j, :], acc[j][:], h1_split[:, 0, j, :].bitcast(F32),
                                  ALU.subtract).then_inc(acc_free[j], 1)
            dve.wait_ge(mm_done, S_T3 + 1)
            dve.tensor_copy(y[:], acc[2][0:1, :]).then_inc(y_set, 1)


def kernel(**inputs):
    import numpy as np
    import concourse.bacc as bacc
    from concourse.bass_utils import run_bass_kernel_spmd

    def chunked(w):
        k, n = w.shape
        return w.reshape(k // P, P, n // P, P).transpose(2, 1, 0, 3).reshape(n // P, P, k)

    def columns(v):
        return v.reshape(-1, P).T

    a = {n: np.asarray(v) for n, v in inputs.items()}
    tables = [a[f"tbl_{f}"] for f in range(NF)]
    sizes = [t.shape[0] for t in tables]
    offsets = [sum(sizes[:f]) for f in range(NF)]
    r = {n: a["L0_rec_" + n] for n in ("Wn1", "bn1", "Wn2", "bn2", "Wa1", "ba1", "Wa2", "ba2", "Wo1", "bo1", "Wo2", "bo2")}
    second = np.stack([chunked(r["Wa2"]), chunked(r["Wo2"])], axis=1).reshape(2 * KT, P, H)
    top2 = chunked(a["W_top2"])
    chunks = np.concatenate([
        chunked(r["Wn1"]), chunked(r["Wn2"]),
        chunked(r["Wa1"][:H]), chunked(r["Wa1"][H:]), chunked(r["Wo1"][:H]), chunked(r["Wo1"][H:]),
        second, chunked(a["W_top1"][:H]), top2.transpose(1, 0, 2).reshape(1, P, H)])
    vectors = np.concatenate([columns(v) for v in (
        r["bn1"], r["bn2"], r["ba1"], r["ba2"], r["bo1"], r["bo2"], a["b_top1"], a["b_top2"], a["W_top3"][:, 0])], axis=1)
    fields = np.concatenate([a["L0_rec_not_idx"], a["L0_rec_and_pairs"].reshape(-1), a["L0_rec_or_pairs"].reshape(-1)])

    arrays = {
        "table": np.concatenate(tables), "ids": a["ids"], "fields": fields, "chunks": chunks, "vectors": vectors,
        "dense": a["dense_ctx"].T, "w_dense": a["W_top1"][H:],
    }
    nc = bacc.Bacc("TRN2", target_bir_lowering=False, num_devices=1)
    arrays = {n: np.ascontiguousarray(v) for n, v in arrays.items()}
    args = [nc.dram_tensor(n, v.shape, mybir.dt.from_np(v.dtype), kind="ExternalInput").ap() for n, v in arrays.items()]
    out = nc.dram_tensor("out", (B, 1), F32, kind="ExternalOutput").ap()
    program(nc, *args, out, offsets)
    return run_bass_kernel_spmd(nc, [arrays], core_ids=[0]).results[0]["out"]
```

```python
from contextlib import ExitStack

import concourse.bass as bass
from concourse import mybir

ALU = mybir.AluOpType
ACT = mybir.ActivationFunctionType
AX = mybir.AxisListType
F32 = mybir.dt.float32
F32R = mybir.dt.float32r
I32 = mybir.dt.int32

P = 128
B = 512
H = 1024
KT = H // P
BT = B // P
NF = 8
NSLOT = 8
NPAIR = 3
NQ = 4
QUAD = P // NQ
QW = H // NQ
NG = B // QUAD
GU = NG // KT
UW = GU * QUAD
BH = B // 2
MB, TB = 4, 4
WR = 4
RR = 3
D1, D2 = 512, 256
KD = 16 + 1

WARM_UP = 39

S_N1, S_N2, S_PAIR, S_L2, S_T1, S_T2, S_T3 = 0, 16, 32, 80, 88, 92, 94
C_N2, C_PAIR, C_L2, C_T1, C_T2 = 16, 24, 72, 88, 92
N_CHUNK = 93
C_SHIFT = 40
U_REST, U_SLOT = 16, 24
V_N1, V_N2, V_A1, V_A2, V_O1, V_O2, V_T2, V_W3 = 0, 8, 16, 24, 32, 40, 48, 50
NV = 52
A0_FROM = 8
REST_AT = {**{g: 1 for g in range(4, 8)}, **{g: 2 + g % 2 for g in range(8, 16)}, 16: 3, 17: 3, 18: 2}
REST_TR = (11, 14, 17, 20)
REST_RING = 3


REST_STEPS, _n = {}, 0
for _g in sorted(REST_AT):
    REST_STEPS[_g] = range(_n, _n + REST_AT[_g])
    _n += REST_AT[_g]


def not_chunk_ahead(g):
    if g < C_N2:
        return g + 3
    u = g % 8
    if u in (0, 5, 6, 7):
        return C_N2 + (g - S_N2) // 8 * 4 + (u - 1 if u else 3)
    return None


def program(nc, table, ids, fields, chunks, vectors, dense, w_dense, out, offsets):
    V = table.shape[0]
    chunk_rows = chunks.rearrange("c p n -> (c p) n")
    quarter_rows = table.rearrange("v (q c) -> (v q) c", q=NQ)

    with ExitStack() as ctx:
        base = (nc.sbuf_base + 63) // 64 * 64
        used = [base]

        def place(name, shape, dt, at=None):
            size = 4
            for n in shape[1:]:
                size *= n
            if at is None:
                at = used[0]
                used[0] += (size + 31) // 32 * 32
            return nc.alloc_sbuf_tensor_at(name, shape, dt, offset=at)

        SPLIT = 2 * KT * B * 4
        area = [used[0] + i * SPLIT for i in range(4)]
        used[0] += 4 * SPLIT
        at_a, at_b, at_c, at_d = area
        xs = [place("x0_split", [P, 2, KT, B], F32R, at_a), place("x1_split", [P, 2, KT, B], F32R, at_b)]
        us = [place("u0_split", [P, 2, KT, B], F32R, at_c), place("u1_split", [P, 2, KT, B], F32R, at_d)]
        not_out = place("not_out", [P, 2, KT, B], F32, at_a)
        slot_split = [place("slot_even", [P, 2, KT, B], F32R, at_b), place("slot_odd", [P, 2, KT, B], F32R, at_c)]
        or_split = place("or_split", [P, 2, KT, B], F32R, at_a)
        and_split = place("and_split", [P, 2, KT, B], F32R, at_b)
        z_split = place("z_split", [P, 2, KT, B], F32R, at_c)
        rows1 = place("rows_input1", [P, NG, KT, QUAD], F32, at_d)
        partial = place("partial", [P, KT, B], F32, at_d)
        and_sum = place("and_sum", [P, KT, B], F32, at_d + SPLIT // 2)
        h1_split = place("h1_split", [P, 2, D1 // P, B], F32R, at_d)
        top2_split = place("top2_split", [P, 2, KT * P], F32R, at_a)
        h2 = place("h2", [P, D2 // P, B], F32, at_d + SPLIT // 2)
        y = place("y", [P, BT], F32, at_d + SPLIT // 2 + D2 // P * B * 4)
        at_rows = used[0]
        rows0 = place("rows_input0", [P, BT, H], F32)
        rest_ring = place("rest_ring", [P, REST_RING, H], F32, at_rows)
        rest_acc = place("rest_acc", [P, H], F32, at_rows + REST_RING * H * 4)
        slot_rows = place("slot_rows", [P, NG, KT, QUAD], F32, at_rows)
        dense_raw = place("dense_raw", [KD, B + D1], F32, at_rows)
        dense_split = place("dense_split", [3 * QUAD, B + D1], F32R, at_rows + (B + D1) * 4)
        z_add = place("z_add", [P, KT, B], F32)
        rest_sum = z_add[:, :, B - P:]
        w_raw = place("w_raw", [P, RR, KT * P], F32)
        w_split = place("w_split", [P, WR, 2, KT * P], F32R)
        ident = place("ident", [P, P], F32)
        vec = place("vec", [P, NV], F32)
        z_bias = place("z_bias", [P, KT], F32)
        ids_sb = place("ids_sb", [P, BT, NF], I32)
        fields_i = place("fields_i", [P, NSLOT], I32)
        fields_f = place("fields_f", [P, NSLOT], F32)
        field_no = place("field_no", [P, NF], F32)
        offs = place("offs", [P, NF], F32)
        row_no = place("row_no", [P, BT, NF], F32)
        onehot = place("onehot", [P, NSLOT, NF], F32)
        picked = place("picked", [P, BT, NF], F32)
        row0 = place("row0", [P, BT], F32)
        row0_idx = place("row0_idx", [P, BT], I32)
        quad_no = place("quad_no", [P, 1], F32)
        row1 = place("row1", [P, NG], F32)
        row1_idx = place("row1_idx", [P, NG], I32)
        at_early = at_d + SPLIT // 2
        picked_q = place("picked_q", [P, 2 * NPAIR, NG, NF], F32, at_early)
        picked1 = place("picked1", [P, NG, NF], F32, at_early + 2 * NPAIR * NG * NF * 4)
        ids_q = place("ids_q", [P, NG, NF], I32, at_early + (2 * NPAIR + 1) * NG * NF * 4)
        row_q = place("row_q", [P, NG, NF], F32, at_early + (2 * NPAIR + 2) * NG * NF * 4)
        slot_row = place("slot_row", [P, 2 * NPAIR, NG], F32)
        slot_idx = place("slot_idx", [P, 2 * NPAIR, NG], I32)
        past_end = place("past_end", [P, 1], F32)
        is_t0 = place("is_t0", [P, NSLOT], F32)
        is_t1 = place("is_t1", [P, NSLOT], F32)
        which_t = place("which_t", [P, NSLOT], I32)
        w_sel = place("w_sel", [P, NSLOT], F32)
        w_emb = place("w_emb", [P, NSLOT], F32)
        paired = place("paired", [P, NF], F32)
        notted = place("notted", [P, NF], F32)
        remain = place("remain", [P, NF], F32)
        w_row = place("w_row", [P, NF], F32)
        rest_row = place("rest_row", [P, BT, NF], F32)
        rest_idx = place("rest_idx", [P, BT, NF], I32)
        w_not = place("w_not", [P, 2, NF], F32)
        w_t = place("w_t", [P, 2], F32)
        not_same = place("not_same", [P, 1], F32)
        n_rest = place("n_rest", [P, 1], F32)
        inv_count = place("inv_count", [P, 1], F32)
        nc.sbuf_tensor("fence", [P, used[0] - nc.sbuf_base], mybir.dt.uint8).__enter__()

        acc = [ctx.enter_context(nc.psum_tensor(f"acc{i}", [P, B], F32)) for i in range(MB)]
        tps = [ctx.enter_context(nc.psum_tensor(f"tps{i}", [P, BT, P], F32)) for i in range(TB)]

        def sem(name):
            return ctx.enter_context(nc.semaphore(name))

        ids_in = sem("ids_in")
        vec_in = sem("vec_in")
        dense_in = sem("dense_in")
        raw_in = [sem(f"raw_in{i}") for i in range(RR)]
        w_hi = sem("w_hi")
        w_lo = sem("w_lo")
        consts_set = sem("consts_set")
        prep = sem("prep")
        idx_set = sem("idx_set")
        quads_in = sem("quads_in")
        rows_in = [sem(f"rows_in{t}") for t in range(BT)]
        slot_in = [sem(f"slot_in{n}") for n in range(KT)]
        tp_done = sem("tp_done")
        selected = sem("selected")
        rest_in = [sem(f"rest_in{r}") for r in range(REST_RING)]
        rest_summed = sem("rest_summed")
        tr_done = sem("tr_done")
        rest_tr = sem("rest_tr")
        tr_free = [sem(f"tr_free{i}") for i in range(TB)]
        op_hi = sem("op_hi")
        mm_done = sem("mm_done")
        acc_free = [sem(f"acc_free{i}") for i in range(MB)]
        hid_hi = sem("hid_hi")
        t_added = sem("t_added")
        pair_in = sem("pair_in")
        and_hi = sem("and_hi")
        and_lo = sem("and_lo")
        or_hi = sem("or_hi")
        z_fin = sem("z_fin")
        z_in = sem("z_in")
        z_hi = sem("z_hi")
        dense_zero = sem("dense_zero")
        dense_hi = sem("dense_hi")
        dense_lo = sem("dense_lo")
        h1_hi = sem("h1_hi")
        y_set = sem("y_set")
        stored = sem("stored")

        def bank_of(h):
            return tps[h % TB][:].rearrange("p t b -> p (t b)")

        def input0_unit(n, part):
            b, m = divmod(n, TB)
            return xs[0][:, part, 2 * m:2 * m + 2, b * BH:(b + 1) * BH], bank_of(n).rearrange("p (k b) -> p k b", k=2)

        def unit_of(s, h, part):
            if s == 0:
                return slot_split[0][:, part, h, :], bank_of(h)
            dst = xs[1] if s < 0 else slot_split[s % 2]
            return dst[:, part, :, h * UW:(h + 1) * UW], bank_of(h).rearrange("p (k b) -> p k b", k=KT)

        block = ctx.enter_context(nc.Block())

        @block.sync
        def _(sp):
            sp.dma_start(ids_sb[:], ids.rearrange("(t p) f -> p t f", p=P)).then_inc(ids_in, 16)
            sp.dma_start(fields_i[:], fields.partition_broadcast(P)).then_inc(ids_in, 16)

            def load(chunk, c, r, split):
                if split is not None:
                    sp.wait_ge(w_lo, split)
                sp.dma_start(w_raw[:, r, :], chunk_rows[bass.ds(chunk * P, P), :]).then_inc(raw_in[r], 16)

            load(0, 0, 0, None)
            for q in range(NQ):
                sp.dma_start(ids_q[q * QUAD:(q + 1) * QUAD], ids.rearrange("(g r) f -> r g f", r=QUAD)).then_inc(quads_in, 16)
            load(1, 1, 1, None)
            load(2, 2, 2, 1)
            sp.dma_start(vec[:], vectors).then_inc(vec_in, 16)
            with sp.Fori(1, C_SHIFT // RR) as i:
                for r in range(RR):
                    load(i * RR + r, i * RR + r, r, i * RR + (r + 1 - RR))
            c = C_SHIFT - 1
            load(c, c, c % RR, c + 1 - RR)
            with sp.Fori(0, (C_T1 - C_SHIFT) // RR) as i:
                for n in range(RR):
                    c = C_SHIFT + n
                    load(i * RR + (c - 2 * KT), i * RR + c, c % RR, i * RR + (c + 1 - RR))
            for c in range(C_T1, N_CHUNK):
                load(c - 2 * KT, c, c % RR, c + 1 - RR)
            sp.wait_ge(y_set, 1)
            sp.dma_start(out.rearrange("(p t) o -> p (t o)", t=BT), y[:]).then_inc(stored, 16)
            sp.wait_ge(stored, 16)

        @block.gpsimd
        def _(pool):
            for f in range(NF):
                pool.memset(offs[:, f:f + 1], float(offsets[f]))
                pool.memset(field_no[:, f:f + 1], float(f))
            pool.memset(ident[:], 0.0).then_inc(consts_set, 1)
            pool.wait_ge(consts_set, 1)
            pool.affine_select(out=ident[:], in_=ident[:], compare_op=ALU.not_equal, fill=1.0, base=0,
                               pattern=[[-1, P]], channel_multiplier=1).then_inc(consts_set, 1)

            for q in range(NQ):
                pool.wait_ge(consts_set, 2 + q)
                pool.memset(quad_no[q * QUAD:(q + 1) * QUAD, :], float(q)).then_inc(consts_set, 1)

            def gather(dst, src, idx, landed):
                pool.indirect_dma_start(dst, None, src, bass.IndirectOffsetOnAxis(ap=idx, axis=0),
                                        bounds_check=src.shape[0] - 1, oob_is_err=False).then_inc(landed, 16)

            pool.wait_ge(idx_set, 1)
            for t in range(BT):
                gather(rows0[:, t, :], table, row0_idx[:, t:t + 1], rows_in[t])
            pool.wait_ge(idx_set, 2)
            for g in range(NG):
                gather(rows1[:, g].rearrange("p k c -> p (k c)"), quarter_rows, row1_idx[:, g:g + 1], slot_in[g // GU])
            pool.wait_ge(idx_set, 3)
            pool.wait_ge(tr_done, KT)
            for n in range(BT * NF):
                r = n % REST_RING
                if n >= REST_RING:
                    pool.wait_ge(rest_summed, n - REST_RING + 1)
                gather(rest_ring[:, r, :], table, rest_idx[:, n // NF, n % NF:n % NF + 1], rest_in[r])
            pool.wait_ge(idx_set, 4)
            pool.wait_ge(rest_tr, 2 * BT)

            for s in range(2 * NPAIR):
                for n in range(KT):
                    if s == 1:
                        pool.wait_ge(tp_done, 2 * KT)
                    elif s > 1:
                        pool.wait_ge(tp_done, s * KT + n + 1)
                    for g in range(GU * n, GU * (n + 1)):
                        gather(slot_rows[:, g].rearrange("p k c -> p (k c)"), quarter_rows,
                               slot_idx[:, s, g:g + 1], slot_in[n])
            pool.wait_ge(tp_done, (1 + 2 * NPAIR) * KT)
            pool.memset(dense_split[:].bitcast(F32), 0.0).then_inc(dense_zero, 1)
            pool.dma_start(dense_raw[:, 0:B], dense).then_inc(dense_in, 16)
            pool.dma_start(dense_raw[:, B:B + D1], w_dense).then_inc(dense_in, 16)

        @block.tensor
        def _(pe):
            def product(bank, w, x, k, wk, start, stop, cols=slice(0, B)):
                lhs = [w[:, p, wk * P:(wk + 1) * P] for p in range(2)]
                for n, (a, b) in enumerate(((0, 0), (0, 1), (1, 0))):
                    ins = pe.matmul(acc[bank][:, cols], lhs[a], x[:, b, k, cols], start=start and n == 0, stop=stop and n == 2)
                return ins

            w_place = [w_split[:, i] for i in range(WR)]

            def input0_blocks(n, half):
                b, m = divmod(n, TB)
                t = 2 * b + half
                for i in range(2):
                    k = 2 * m + i
                    ins = pe.transpose(tps[m][:, 2 * i + half, :], rows0[:, t, k * P:(k + 1) * P], ident[:])
                if half == 1:
                    ins.then_inc(tr_done, 1)

            def rest_units(t):
                pe.wait_ge(rest_summed, NF * (t + 1))
                for q in range(2):
                    n = U_REST + 2 * t + q
                    pe.wait_ge(tr_free[n % TB], n // TB)
                    for i in range(4):
                        ins = pe.transpose(tps[n % TB][:, i, :], rest_sum[:, 4 * q + i, :], ident[:])
                    ins.then_inc(rest_tr, 1)

            pe.wait_ge(consts_set, 2)
            for _ in range(WARM_UP):
                pe.transpose(tps[TB - 1][:, 0, :], ident[:], ident[:])
            for half in range(2):
                pe.wait_ge(rows_in[half], 16)
                for n in range(TB):
                    input0_blocks(n, half)
            for b in range(2):
                for m in range(TB):
                    if b == 0 and m >= 2:
                        for n in (2 * m, 2 * m + 1):
                            pe.wait_ge(tr_free[n % TB], 1)
                            for half in range(2):
                                if n == TB:
                                    pe.wait_ge(rows_in[2 + half], 16)
                                input0_blocks(n, half)
                    pe.wait_ge(tr_free[m], b + 1)
                    for g in range(2):
                        if b + m == 0:
                            pe.wait_ge(w_lo, g + 1)
                        for k in (2 * m, 2 * m + 1):
                            ins = product(g, w_place[g], xs[0], k, k, k == 0, k == KT - 1, slice(b * BH, (b + 1) * BH))
                        if b == 1 and m == TB - 1:
                            ins.then_inc(mm_done, 1)
            for g in range(2, S_N2):
                if g in REST_TR:
                    rest_units(REST_TR.index(g))
                pe.wait_ge(w_lo, g + 1)
                if g >= MB:
                    pe.wait_ge(acc_free[g % MB], g // MB)
                if g == KT:
                    pe.wait_ge(tr_free[TB - 1], U_REST // TB)
                for k in range(KT):
                    ins = product(g % MB, w_place[g % WR], xs[g // KT], k, k, k == 0, k == KT - 1)
                ins.then_inc(mm_done, 1)

            for g in range(16):
                f, c = g % 8 // 4, C_N2 + g // 8 * 4 + g % 4
                if S_N2 + g in REST_TR:
                    rest_units(REST_TR.index(S_N2 + g))
                pe.wait_ge(acc_free[MB - 1], 2 * (f + 1))
                pe.wait_ge(w_lo, c + 1)
                pe.wait_ge(acc_free[g % MB], (S_N2 + g) // MB)
                for k in range(KT):
                    ins = product(g % MB, w_place[c % WR], us[f], k, k, k == 0, k == KT - 1)
                ins.then_inc(mm_done, 1)

            def slot_steps(s, par, by_blocks=False):
                for h in range(KT):
                    pe.wait_ge(w_lo, s * KT + (C_PAIR + h + 1))
                    pe.wait_ge(acc_free[h % MB], s * 2 + (S_PAIR + h) // MB)
                    for k in range(KT):
                        if h == 0 and by_blocks:
                            if k == 0:
                                pe.wait_ge(tr_free[0], (U_SLOT + 4) // TB + 1)
                            elif k >= 5:
                                pe.wait_ge(tr_free[k % TB], (U_SLOT + k) // TB + 1)
                        elif h == 0 and k == 0:
                            pe.wait_ge(tr_free[TB - 1], s * 2 + ((U_SLOT + KT - 1) // TB + 1))
                        ins = product(h % MB, w_place[(C_PAIR + h) % WR], slot_split[par], k, k, k == 0, k == KT - 1)
                    ins.then_inc(mm_done, 1)

            slot_steps(0, 0, by_blocks=True)
            slot_steps(1, 1)
            with pe.Fori(1, NPAIR) as i:
                slot_steps(i * 2, 0)
                slot_steps(i * 2 + 1, 1)

            with pe.Fori(0, 2) as hh:
                for u in range(4):
                    pe.wait_ge(acc_free[u], hh + S_L2 // MB)
                    for part, x in enumerate((and_split, or_split)):
                        w = 2 * u + part
                        pe.wait_ge(w_lo, hh * 8 + (C_L2 + w + 1))
                        for k in range(KT):
                            if part == 0 and k == 0:
                                pe.wait_ge(and_lo, KT)
                            if part == 1 and k in (0, KT - 1):
                                pe.wait_ge(acc_free[2 + k // (KT - 1)], S_L2 // MB)
                            ins = product(u, w_place[w % WR], x, k, k, part + k == 0, part == 1 and k == KT - 1)
                    ins.then_inc(mm_done, 1)

            for j in range(D1 // P):
                pe.wait_ge(w_lo, C_T1 + j + 1)
                pe.wait_ge(acc_free[j], (S_T1 + j) // MB)
                pe.wait_ge(acc_free[2], S_T1 // MB)
                for k in range(KT - 1):
                    product(j, w_place[j], z_split, k, k, k == 0, False)
            pe.wait_ge(dense_lo, 1)
            pe.wait_ge(acc_free[3], S_T1 // MB)
            for j in range(D1 // P):
                product(j, w_place[j], z_split, KT - 1, KT - 1, False, False)
                pe.matmul(acc[j][:], dense_split[:, B + j * P:B + (j + 1) * P], dense_split[:, 0:B],
                          start=False, stop=True).then_inc(mm_done, 1)

            K2 = D1 // P
            pe.wait_ge(w_lo, C_T2 + 1)
            for j in range(D2 // P):
                pe.wait_ge(acc_free[j], S_T2 // MB)
                for k in range(K2):
                    if j == 0:
                        pe.wait_ge(acc_free[k], S_T2 // MB)
                    ins = product(j, top2_split[:], h1_split, k, j * K2 + k, k == 0, k == K2 - 1)
                ins.then_inc(mm_done, 1)

            pe.wait_ge(vec_in, 16)
            for k in range(D2 // P):
                pe.wait_ge(acc_free[2 + k], S_T3 // MB)
                pe.wait_ge(acc_free[k], S_T2 // MB + 1)
                for t in range(BT):
                    ins = pe.matmul(acc[2 + k][:, t:t + 1], h2[:, k, :].rearrange("p (b t) -> p t b", t=BT)[:, t, :],
                                    vec[:, V_W3 + k:V_W3 + k + 1], start=True, stop=True)
                ins.then_inc(mm_done, 1)

        @block.scalar
        def _(act):
            def chunk_hi(c, steps, dst=None):
                dst = w_split[:, c % WR] if dst is None else dst
                act.wait_ge(raw_in[c % RR], 16 * (c // RR + 1))
                if steps > 0:
                    act.wait_ge(mm_done, steps)
                act.copy(dst[:, 0, :], w_raw[:, c % RR, :]).then_inc(w_hi, 1)

            def slot_operand_hi(s, h):
                if s < 0:
                    act.wait_ge(tp_done, h + 1)
                else:
                    act.wait_ge(selected, s * KT + h + 1)
                dst, bank = unit_of(s, h, 0)
                act.copy(dst, bank).then_inc(op_hi, 1)

            for c in range(2):
                chunk_hi(c, 0)
            for n in range(KT):
                if n == TB:
                    chunk_hi(2, 0)
                act.wait_ge(tr_done, n + 1)
                dst, bank = input0_unit(n, 0)
                act.copy(dst, bank).then_inc(op_hi, 1)
            act.wait_ge(vec_in, 16)

            def move_rest(t):
                for q in range(2):
                    n = U_REST + 2 * t + q
                    act.wait_ge(rest_tr, 2 * t + q + 1)
                    act.copy(z_add[:, 4 * q:4 * q + 4, t * P:(t + 1) * P], tps[n % TB][:]).then_inc(tr_free[n % TB], 1)

            for g in range(S_N2):
                f, j = divmod(g, KT)
                chunk_hi(not_chunk_ahead(g), g)
                if f == 0:
                    slot_operand_hi(-1, g)
                if g in REST_TR:
                    move_rest(REST_TR.index(g))
                act.wait_ge(mm_done, g + 1)
                bias = vec[:, V_N1 + j:V_N1 + j + 1]
                act.activation(us[f][:, 0, j, :], acc[g % MB][:], ACT.Relu, bias=bias)
                act.activation(acc[g % MB][:], acc[g % MB][:], ACT.Relu, bias=bias).then_inc(hid_hi, 1)

            for g in range(16):
                f, j = g % 8 // 4, g // 8 * 4 + g % 4
                c = not_chunk_ahead(S_N2 + g)
                if c is not None:
                    chunk_hi(c, S_N2 + g)
                if S_N2 + g in REST_TR:
                    move_rest(REST_TR.index(S_N2 + g))
                act.wait_ge(mm_done, S_N2 + g + 1)
                act.activation(not_out[:, f, j, :], acc[g % MB][:], ACT.Tanh,
                               bias=vec[:, V_N2 + j:V_N2 + j + 1]).then_inc(acc_free[g % MB], 1)
                if g >= A0_FROM:
                    slot_operand_hi(0, g - A0_FROM)

            def read_out(n):
                s, h = divmod(n, KT)
                if s % 2 == 0:
                    bias = vec[:, (V_A1, V_A1, V_O1)[s // 2] + h:][:, 0:1]
                    act.wait_ge(mm_done, S_PAIR + n + 1)
                    act.activation(partial[:, h, :], acc[h % MB][:], ACT.Identity, bias=bias).then_inc(acc_free[h % MB], 1)
                elif s == 1:
                    act.wait_ge(pair_in, h + 1)
                    act.activation(and_sum[:, h, :], acc[h % MB][:], ACT.Relu).then_inc(acc_free[h % MB], 1)

            for n in range(5 * KT):
                s, h = divmod(n, KT)
                chunk_hi(C_PAIR + n + 3, S_PAIR + n)
                if n > 0:
                    read_out(n - 1)
                slot_operand_hi(s + 1, h)
            read_out(5 * KT - 1)
            act.wait_ge(mm_done, S_PAIR + 5 * KT)
            act.wait_ge(acc_free[MB - 1], (S_PAIR + 4 * KT) // MB)
            for h in range(KT):
                if h < KT - 1:
                    chunk_hi(C_PAIR + 5 * KT + h + 3, S_PAIR + 5 * KT + h)
                act.copy(and_split[:, 0, h, :], and_sum[:, h, :]).then_inc(and_hi, 1)
                act.wait_ge(pair_in, 2 * KT + h + 1)
                act.activation(or_split[:, 0, h, :], acc[h % MB][:], ACT.Relu).then_inc(or_hi, 1)

            for j in range(KT):
                for c in (C_L2 + 2 + 2 * j, C_L2 + 3 + 2 * j):
                    chunk_hi(c, S_L2 + j)
                if j == 4:
                    act.wait_ge(dense_in, 32)
                    act.wait_ge(dense_zero, 1)
                    act.copy(dense_split[0:KD, :], dense_raw[:])
                    act.copy(dense_split[QUAD:QUAD + KD, 0:B], dense_raw[:, 0:B])
                    act.copy(dense_split[2 * QUAD:2 * QUAD + KD, B:], dense_raw[:, B:]).then_inc(dense_hi, 1)
                act.wait_ge(z_in, j + 1)
                act.copy(z_split[:, 0, j, :], acc[j % MB][:]).then_inc(z_hi, 1)
            for c in (C_T1 + 2, C_T1 + 3):
                chunk_hi(c, S_T1)
            chunk_hi(C_T2, S_T1, top2_split[:])
            for j in range(D1 // P):
                act.wait_ge(mm_done, S_T1 + j + 1)
                act.activation(h1_split[:, 0, j, :], acc[j][:], ACT.Relu).then_inc(h1_hi, 1)
            for j in range(D2 // P):
                act.wait_ge(mm_done, S_T2 + j + 1)
                act.activation(h2[:, j, :], acc[j][:], ACT.Relu,
                               bias=vec[:, V_T2 + j:V_T2 + j + 1]).then_inc(acc_free[j], 1)

        @block.vector
        def _(dve):
            links = [0]

            def link(ins):
                links[0] += 1
                ins.then_inc(prep, 1)
                dve.wait_ge(prep, links[0])

            dve.wait_ge(consts_set, 1)
            dve.wait_ge(ids_in, 32)
            dve.tensor_copy(fields_f[:], fields_i[:])
            link(dve.tensor_tensor(row_no[:], ids_sb[:], offs[:].unsqueeze(1).broadcast_to([P, BT, NF]), ALU.add))
            link(dve.scalar_tensor_tensor(out=picked[:], in0=field_no[:].unsqueeze(1).broadcast_to([P, BT, NF]),
                                          scalar=fields_f[:, 0:1], in1=row_no[:], op0=ALU.is_equal, op1=ALU.mult))
            link(dve.tensor_reduce(row0[:], picked[:], AX.X, ALU.add))
            dve.tensor_copy(row0_idx[:], row0[:]).then_inc(idx_set, 1)
            dve.tensor_tensor(onehot[:], fields_f[:].unsqueeze(2).broadcast_to([P, NSLOT, NF]),
                              field_no[:].unsqueeze(1).broadcast_to([P, NSLOT, NF]), ALU.is_equal)
            dve.wait_ge(quads_in, 16 * NQ)
            link(dve.tensor_tensor(row_q[:], ids_q[:], offs[:].unsqueeze(1).broadcast_to([P, NG, NF]), ALU.add))
            link(dve.tensor_tensor(picked1[:], onehot[:, 1:2, :].broadcast_to([P, NG, NF]), row_q[:], ALU.mult))
            link(dve.tensor_reduce(row1[:], picked1[:], AX.X, ALU.add))
            dve.wait_ge(consts_set, 2 + NQ)
            dve.tensor_scalar(row1_idx[:], row1[:], float(NQ), quad_no[:, 0:1], ALU.mult, ALU.add).then_inc(idx_set, 1)

            def chunk_lo(c, dst=None):
                dst = w_split[:, c % WR] if dst is None else dst
                dve.wait_ge(w_hi, c + 1)
                dve.tensor_tensor(dst[:, 1, :], w_raw[:, c % RR, :], dst[:, 0, :].bitcast(F32), ALU.subtract).then_inc(w_lo, 1)

            for c in range(2):
                chunk_lo(c)
            for n in range(KT):
                if n == TB:
                    chunk_lo(2)
                dve.wait_ge(op_hi, n + 1)
                hi, bank = input0_unit(n, 0)
                dve.tensor_tensor(input0_unit(n, 1)[0], bank, hi.bitcast(F32), ALU.subtract).then_inc(tr_free[n % TB], 1)

            dve.tensor_reduce(paired[:], onehot[:, 2:NSLOT, :].rearrange("p s f -> p f s"), AX.X, ALU.max)
            link(dve.tensor_tensor(notted[:], onehot[:, 0, :], onehot[:, 1, :], ALU.max))
            link(dve.tensor_scalar(remain[:], paired[:], -1.0, 1.0, ALU.mult, ALU.add))
            link(dve.tensor_tensor(w_row[:], remain[:], notted[:], ALU.is_gt))
            link(dve.tensor_scalar(rest_row[:].rearrange("p t f -> p f t"),
                                   w_row[:].unsqueeze(2).broadcast_to([P, NF, BT]), -float(V), float(V), ALU.mult, ALU.add))
            dve.tensor_tensor(rest_idx[:], rest_row[:], row_no[:], ALU.add).then_inc(idx_set, 1)

            pairs = (P, 2 * NPAIR, NG)
            link(dve.tensor_tensor(picked_q[:], onehot[:, 2:].unsqueeze(2).broadcast_to([*pairs, NF]),
                                   row_q[:].unsqueeze(1).broadcast_to([*pairs, NF]), ALU.mult))
            dve.tensor_reduce(slot_row[:], picked_q[:], AX.X, ALU.add)
            dve.tensor_scalar(past_end[:], quad_no[:], float(NQ * (V - 1)), None, ALU.add)
            dve.tensor_scalar(is_t0[:], fields_f[:], fields_f[:, 0:1], None, ALU.is_equal)
            dve.tensor_scalar(is_t1[:], fields_f[:], fields_f[:, 1:2], None, ALU.is_equal)
            link(dve.tensor_scalar(which_t[:], fields_f[:], fields_f[:, 1:2], None, ALU.is_equal))
            link(dve.tensor_tensor(w_sel[:], is_t0[:], is_t1[:], ALU.max))
            link(dve.tensor_scalar(w_emb[:], w_sel[:], -1.0, 1.0, ALU.mult, ALU.add))
            link(dve.scalar_tensor_tensor(out=slot_row[:], in0=slot_row[:], scalar=float(1 - V),
                                          in1=w_emb[:, 2:].unsqueeze(2).broadcast_to(pairs), op0=ALU.add, op1=ALU.mult))
            dve.tensor_scalar(slot_idx[:], slot_row[:], float(NQ), past_end[:, 0:1], ALU.mult, ALU.add).then_inc(idx_set, 1)
            dve.tensor_reduce(n_rest[:], remain[:], AX.X, ALU.add)
            dve.tensor_scalar(not_same[:], is_t0[:, 1:2], -1.0, 1.0, ALU.mult, ALU.add)
            link(dve.tensor_tensor(w_not[:], onehot[:, 0:2, :], remain[:].unsqueeze(1).broadcast_to([P, 2, NF]), ALU.mult))
            link(dve.tensor_reduce(w_t[:], w_not[:], AX.X, ALU.add))
            dve.tensor_scalar(w_t[:, 1:2], w_t[:, 1:2], not_same[:, 0:1], None, ALU.mult)
            link(dve.tensor_scalar(n_rest[:], n_rest[:], float(NPAIR), None, ALU.add))
            link(dve.reciprocal(inv_count[:], n_rest[:]))
            dve.wait_ge(vec_in, 16)
            link(dve.scalar_tensor_tensor(out=z_bias[:], in0=vec[:, V_A2:V_A2 + KT], scalar=2.0,
                                          in1=vec[:, V_O2:V_O2 + KT], op0=ALU.mult, op1=ALU.add))
            link(dve.tensor_scalar(z_bias[:], z_bias[:], inv_count[:, 0:1], None, ALU.mult))

            def rest_sums(g):
                for n in REST_STEPS.get(g, ()):
                    t, fld = divmod(n, NF)
                    row, w = rest_ring[:, n % REST_RING, :], w_row[:, fld:fld + 1]
                    dve.wait_ge(rest_in[n % REST_RING], 16 * (n // REST_RING + 1))
                    if n > 0:
                        dve.wait_ge(rest_summed, n)
                    if fld == 0:
                        ins = dve.tensor_scalar(rest_acc[:], row, w, None, ALU.mult)
                    elif fld < NF - 1:
                        ins = dve.scalar_tensor_tensor(out=rest_acc[:], in0=row, scalar=w, in1=rest_acc[:],
                                                       op0=ALU.mult, op1=ALU.add)
                    else:
                        if t >= 1:
                            dve.wait_ge(rest_tr, 2 * t)
                        for q in range(NQ):
                            part = slice(q * QW, (q + 1) * QW)
                            ins = dve.scalar_tensor_tensor(
                                out=rest_sum[:, :, q * QUAD:(q + 1) * QUAD],
                                in0=row[:, part].rearrange("p (k c) -> p k c", k=KT), scalar=w,
                                in1=rest_acc[:, part].rearrange("p (k c) -> p k c", k=KT), op0=ALU.mult, op1=ALU.add)
                    ins.then_inc(rest_summed, 1)

            def transpose(s, h):
                dve.wait_ge(tr_free[h % TB], (U_SLOT + s * KT + h if s >= 0 else KT + h) // TB)
                if s == 0:
                    for n in range(KT if h == 0 else 0):
                        dve.wait_ge(slot_in[n], 16 * GU * 2)
                    src, dst = slot_rows[:, :, h, :], bank_of(h).rearrange("p (g r) -> p g r", g=NG)
                else:
                    dve.wait_ge(slot_in[h], 16 * GU * (s + 2))
                    src = (rows1 if s < 0 else slot_rows)[:, h * GU:(h + 1) * GU]
                    dst = bank_of(h).rearrange("p (k g r) -> p g k r", k=KT, g=GU)
                dve.transpose(dst, src).then_inc(tp_done, 1)

            def select(s, h):
                dve.wait_ge(tp_done, (s + 1) * KT + h + 1)
                bank = unit_of(s, h, 0)[1]
                blocks = not_out[:].rearrange("p m k b -> p (m k) b")
                if s == 0:
                    bank, result = bank.unsqueeze(1), blocks[:, bass.ds(which[s] * KT + h, 1), :]
                else:
                    result = blocks[:, bass.ds(which[s] * KT, KT), h * UW:(h + 1) * UW]
                dve.scalar_tensor_tensor(out=bank, in0=result, scalar=w_sel[:, 2 + s:3 + s], in1=bank,
                                         op0=ALU.mult, op1=ALU.add).then_inc(selected, 1)

            def slot_operand_lo(s, h):
                dve.wait_ge(op_hi, (s + 2) * KT + h + 1)
                hi, bank = unit_of(s, h, 0)
                dve.tensor_tensor(unit_of(s, h, 1)[0], bank, hi.bitcast(F32), ALU.subtract).then_inc(tr_free[h % TB], 1)

            for g in range(S_N2):
                f, j = divmod(g, KT)
                if f == 0:
                    transpose(-1, g)
                chunk_lo(not_chunk_ahead(g))
                if f == 0:
                    slot_operand_lo(-1, g)
                rest_sums(g)
                dve.wait_ge(hid_hi, g + 1)
                dve.tensor_tensor(us[f][:, 1, j, :], acc[g % MB][:], us[f][:, 0, j, :].bitcast(F32), ALU.subtract)\
                    .then_inc(acc_free[g % MB], 1)

            which = [dve.value_load(which_t[0:1, 2 + s:3 + s], min_val=0, max_val=1) for s in range(2 * NPAIR)]
            for g in range(16):
                c = not_chunk_ahead(S_N2 + g)
                if c is not None:
                    chunk_lo(c)
                rest_sums(S_N2 + g)
                if g >= A0_FROM:
                    h = g - A0_FROM
                    if h == 0:
                        for n in range(TB):
                            transpose(0, n)
                    last = S_N2 + h // 4 * 8 + 4 + h % 4
                    dve.wait_ge(acc_free[last % MB], last // MB + 1)
                    select(0, h)
                    slot_operand_lo(0, h)
                    if h < TB:
                        transpose(0, h + TB)

            def add_not_result(f, j):
                if j == 0 and f == 1:
                    dve.wait_ge(t_added, KT)
                dve.scalar_tensor_tensor(out=z_add[:, j, :], in0=not_out[:, f, j, :], scalar=w_t[:, f:f + 1],
                                         in1=z_add[:, j, :], op0=ALU.mult, op1=ALU.add).then_inc(t_added, 1)

            def add_partial(s, h):
                dve.wait_ge(mm_done, s * KT + (S_PAIR + h + 1))
                dve.wait_ge(acc_free[h % MB], s * 2 + ((S_PAIR - KT + h) // MB + 1))
                dve.tensor_tensor(acc[h % MB][:], acc[h % MB][:], partial[:, h, :], ALU.add).then_inc(pair_in, 1)

            def finish_pair(n):
                s, h = divmod(n, KT)
                if s % 2 == 1:
                    add_partial(s, h)
                if s == 3:
                    dve.wait_ge(acc_free[h % MB], (S_PAIR + KT + h) // MB + 1)
                    dve.wait_ge(pair_in, KT + h + 1)
                    dve.scalar_tensor_tensor(out=and_sum[:, h, :], in0=acc[h % MB][:], scalar=0.0,
                                             in1=and_sum[:, h, :], op0=ALU.max, op1=ALU.add)\
                        .then_inc(acc_free[h % MB], 1)

            transpose(1, 0)
            select(1, 0)
            for n in range(5 * KT):
                s, h = divmod(n, KT)
                if n > 0:
                    finish_pair(n - 1)
                chunk_lo(C_PAIR + n + 3)
                if n < 5 * KT - 1:
                    transpose(*divmod(n + KT + 1, KT))
                slot_operand_lo(s + 1, h)
                if s in (0, 2):
                    add_not_result(s // 2, h)
                if n < 5 * KT - 1:
                    select(*divmod(n + KT + 1, KT))
            for h in range(KT):
                if h < KT - 1:
                    chunk_lo(C_PAIR + 5 * KT + h + 3)
                dve.wait_ge(and_hi, h + 1)
                dve.tensor_tensor(and_split[:, 1, h, :], and_sum[:, h, :], and_split[:, 0, h, :].bitcast(F32),
                                  ALU.subtract).then_inc(and_lo, 1)
                dve.wait_ge(t_added, 2 * KT)
                dve.tensor_scalar(z_add[:, h, :], z_add[:, h, :], inv_count[:, 0:1], z_bias[:, h:h + 1],
                                  ALU.mult, ALU.add).then_inc(z_fin, 1)
                add_partial(5, h)
                dve.wait_ge(or_hi, h + 1)
                dve.scalar_tensor_tensor(out=or_split[:, 1, h, :], in0=acc[h % MB][:], scalar=0.0,
                                         in1=or_split[:, 0, h, :].bitcast(F32), op0=ALU.max, op1=ALU.subtract)\
                    .then_inc(acc_free[h % MB], 1)

            for j in range(KT):
                for c in (C_L2 + 2 + 2 * j, C_L2 + 3 + 2 * j):
                    chunk_lo(c)
                if j == 4:
                    dve.wait_ge(dense_hi, 1)
                    hi = dense_split[0:KD, :].bitcast(F32)
                    dve.tensor_tensor(dense_split[2 * QUAD:2 * QUAD + KD, 0:B], dense_raw[:, 0:B], hi[:, 0:B], ALU.subtract)
                    dve.tensor_tensor(dense_split[QUAD:QUAD + KD, B:], dense_raw[:, B:], hi[:, B:], ALU.subtract)\
                        .then_inc(dense_lo, 1)
                dve.wait_ge(z_fin, j + 1)
                dve.wait_ge(mm_done, S_L2 + j + 1)
                dve.scalar_tensor_tensor(out=acc[j % MB][:], in0=acc[j % MB][:], scalar=inv_count[:, 0:1],
                                         in1=z_add[:, j, :], op0=ALU.mult, op1=ALU.add).then_inc(z_in, 1)
                dve.wait_ge(z_hi, j + 1)
                dve.tensor_tensor(z_split[:, 1, j, :], acc[j % MB][:], z_split[:, 0, j, :].bitcast(F32),
                                  ALU.subtract).then_inc(acc_free[j % MB], 1)
            for c in (C_T1 + 2, C_T1 + 3):
                chunk_lo(c)
            chunk_lo(C_T2, top2_split[:])
            for j in range(D1 // P):
                dve.wait_ge(h1_hi, j + 1)
                dve.scalar_tensor_tensor(out=h1_split[:, 1, j, :], in0=acc[j][:], scalar=0.0,
                                         in1=h1_split[:, 0, j, :].bitcast(F32), op0=ALU.max, op1=ALU.subtract)\
                    .then_inc(acc_free[j], 1)
            dve.wait_ge(mm_done, S_T3 + 1)
            link(dve.tensor_copy(y[:], acc[2][:, 0:BT]))
            dve.wait_ge(mm_done, S_T3 + 2)
            dve.tensor_tensor(y[:], acc[3][:, 0:BT], y[:], ALU.add).then_inc(y_set, 1)


def kernel(**inputs):
    import numpy as np
    import concourse.bacc as bacc
    from concourse.bass_utils import run_bass_kernel_spmd

    def chunked(w):
        k, n = w.shape
        return w.reshape(k // P, P, n // P, P).transpose(2, 1, 0, 3).reshape(n // P, P, k)

    def columns(v):
        return v.reshape(-1, P).T

    def embedding_order(w, axis=0):
        shape = list(w.shape)
        w = w.reshape(shape[:axis] + [NQ, KT, QUAD] + shape[axis + 1:]).swapaxes(axis, axis + 1)
        return w.reshape(shape)

    a = {n: np.asarray(v) for n, v in inputs.items()}
    tables = [a[f"tbl_{f}"] for f in range(NF)]
    sizes = [t.shape[0] for t in tables]
    offsets = [sum(sizes[:f]) for f in range(NF)]
    r = {n: a["L0_rec_" + n] for n in ("Wn1", "bn1", "Wn2", "bn2", "Wa1", "ba1", "Wa2", "ba2", "Wo1", "bo1", "Wo2", "bo2")}
    for n in ("Wn2", "Wa2", "Wo2"):
        r[n] = embedding_order(r[n], 1)
    for n in ("bn2", "ba2", "bo2"):
        r[n] = embedding_order(r[n])
    second = np.stack([chunked(r["Wa2"]), chunked(r["Wo2"])], axis=1).reshape(2 * KT, P, H)
    top2 = chunked(a["W_top2"])
    chunks = np.concatenate([
        chunked(r["Wn1"]), chunked(embedding_order(r["Wn1"])), chunked(r["Wn2"]),
        *(chunked(embedding_order(w)) for w in (r["Wa1"][:H], r["Wa1"][H:], r["Wo1"][:H], r["Wo1"][H:])),
        second, chunked(embedding_order(a["W_top1"][:H])), top2.transpose(1, 0, 2).reshape(1, P, H)])
    vectors = np.concatenate([columns(v) for v in (
        r["bn1"], r["bn2"], r["ba1"], r["ba2"], r["bo1"], r["bo2"], a["b_top2"], a["W_top3"][:, 0])], axis=1)
    fields = np.concatenate([a["L0_rec_not_idx"], a["L0_rec_and_pairs"].reshape(-1), a["L0_rec_or_pairs"].reshape(-1)])

    arrays = {
        "table": np.concatenate([*tables, np.zeros((1, H), tables[0].dtype)]),
        "ids": a["ids"], "fields": fields, "chunks": chunks, "vectors": vectors,
        "dense": np.concatenate([a["dense_ctx"].T, np.ones((1, B), a["dense_ctx"].dtype)]),
        "w_dense": np.concatenate([a["W_top1"][H:], a["b_top1"][None]]),
    }
    nc = bacc.Bacc("TRN2", target_bir_lowering=False, num_devices=1)
    arrays = {n: np.ascontiguousarray(v) for n, v in arrays.items()}
    args = [nc.dram_tensor(n, v.shape, mybir.dt.from_np(v.dtype), kind="ExternalInput").ap() for n, v in arrays.items()]
    out = nc.dram_tensor("out", (B, 1), F32, kind="ExternalOutput").ap()
    program(nc, *args, out, offsets)
    return run_bass_kernel_spmd(nc, [arrays], core_ids=[0]).results[0]["out"]
```
